# Optimizing a Trainium2 kernel written in Bass

```python
import numpy as np
import jax
import jax.numpy as jnp

def _softmax(x, axis=-1):
    return jax.nn.softmax(x, axis=axis)

def _gelu(x):
    return jax.nn.gelu(x, approximate=True)

def _silu(x):
    return jax.nn.silu(x)

def _sigmoid(x):
    return jax.nn.sigmoid(x)

def _layernorm(x, axis=-1, eps=1e-05):
    m = jnp.mean(x, axis=axis, keepdims=True)
    v = jnp.var(x, axis=axis, keepdims=True)
    return (x - m) / jnp.sqrt(v + eps)

def _scatter_add(tgt, idx, src, axis=0):
    return tgt.at[idx].add(src)

def _segment_sum(src, seg, n):
    return jax.ops.segment_sum(src, seg, n)
kernel_name = 'mk_decoder_postln_d2_seqx_r8_f597c8'

def setup_inputs(seed: int=0):
    np.random.seed(seed)
    _w = jnp.asarray

    def _rec_inputs():
        import jax
        import jax.numpy as jnp
        _rk = jax.random.key(seed)
        x = -0.0002928 + 1 * jax.random.normal(jax.random.fold_in(_rk, 1), (32, 128, 128), jnp.float32)
        _lenS = 128 - jax.random.randint(jax.random.fold_in(_rk, 7), (32,), 0, max(1, 128 // 4) + 1, jnp.int32)
        _lenS2 = 128 - jax.random.randint(jax.random.fold_in(_rk, 8), (32,), 0, max(1, 128 // 4) + 1, jnp.int32)
        _ctx_1024P = jax.random.normal(jax.random.fold_in(_rk, 11), (32, 16, 128), jnp.float32)
        _ctx_1024c = jax.random.dirichlet(jax.random.fold_in(_rk, 511), 0.3 * jnp.ones((16,), jnp.float32), (32, 128))
        _ctx_1024t = jnp.einsum('bsk,bkd->bsd', _ctx_1024c, _ctx_1024P)
        _ctx_1024t = _ctx_1024t * jax.lax.rsqrt(jnp.mean(jnp.square(_ctx_1024t)) + 1e-12) * 0.953939
        ctx_1024 = -1.39393e-06 + 0.999914 * (_ctx_1024t + 0.3 * jax.random.normal(jax.random.fold_in(_rk, 611), (32, 128, 128), jnp.float32))
        return (x, ctx_1024)
    x, ctx_1024 = _rec_inputs()

    def _L0_attn_setup():
        import jax, jax.numpy as jnp
        import numpy as np
        B, N, DE, H, DH = (2, 128, 128, 16, 64)
        DK = H * DH
        MIN_EXP = -30.0
        EPS = 0.0001
        key = jax.random.key(seed)
        ks = jax.random.split(key, 8)

        def g(i, shape, sc=1.0):
            return jax.random.normal(ks[i], shape, jnp.float32) * sc
        freqs = 10000.0 ** (-np.arange(DH // 2, dtype=np.float64) / (DH // 2))
        omega = jnp.asarray(np.tile(freqs[None, :], (H, 1)), jnp.float32)
        return {'x': g(0, (B, N, DE)), 'Wq': g(1, (DE, 2 * DK), 1.0 / np.sqrt(DE)), 'Wk': g(2, (DE, 2 * DK), 1.0 / np.sqrt(DE)), 'Wv': g(3, (DE, 2 * DK), 1.0 / np.sqrt(DE)), 'Wo': g(4, (2 * DK, DE), 1.0 / np.sqrt(2 * DK)), 'omega': omega, 'mu_raw': g(5, (H,)) - 2.0, 'sigma_raw': g(6, (H,)), 'eta_raw': jnp.ones((H,), jnp.float32), 'gamma_raw': jnp.ones((H,), jnp.float32), 'tau': jnp.ones((H,), jnp.float32), 'nu_raw': jnp.ones((H,), jnp.float32) * 4.0}
    _L0_attn_all = _L0_attn_setup()
    _L0_attn_in = {k: v for k, v in _L0_attn_all.items() if k in ('Wq', 'Wk', 'Wv', 'Wo', 'omega', 'mu_raw', 'sigma_raw', 'eta_raw', 'gamma_raw', 'tau', 'nu_raw')}
    del _L0_attn_all

    def _L0_xattn_setup():
        import jax, jax.numpy as jnp
        import numpy as np
        B, S, D, NH = (2, 256, 128, 8)
        DH = D // NH
        EPS = 1e-06
        LN_EPS = 1e-05

        def _mlstm_cell(q, k, v, igate_w, igate_b, fgate_w, fgate_b, ln_scale):
            Slen = q.shape[0]
            ifg = jnp.concatenate([q, k, v], axis=-1)
            ig = (ifg @ igate_w.T + igate_b).T
            fg = (ifg @ fgate_w.T + fgate_b).T
            qh = q.reshape(Slen, NH, DH).transpose(1, 0, 2)
            kh = k.reshape(Slen, NH, DH).transpose(1, 0, 2)
            vh = v.reshape(Slen, NH, DH).transpose(1, 0, 2)
            log_f = jax.nn.log_sigmoid(fg)
            cs = jnp.cumsum(log_f, axis=1)
            fg_mat = cs[:, :, None] - cs[:, None, :]
            mask = jnp.tril(jnp.ones((Slen, Slen), dtype=bool))
            log_fg_mat = jnp.where(mask, fg_mat, -jnp.inf)
            log_D = log_fg_mat + ig[:, None, :]
            max_log_D = jnp.max(log_D, axis=-1, keepdims=True)
            D_mat = jnp.exp(log_D - max_log_D)
            qk = jnp.einsum('hsd,htd->hst', qh, kh) / np.sqrt(DH)
            C = qk * D_mat
            normalizer = jnp.maximum(jnp.abs(C.sum(axis=-1, keepdims=True)), jnp.exp(-max_log_D))
            h = jnp.einsum('hst,htd->hsd', C / (normalizer + EPS), vh)
            h = h.transpose(1, 0, 2).reshape(Slen, D)
            mu = h.mean(axis=-1, keepdims=True)
            var = h.var(axis=-1, keepdims=True)
            return (h - mu) / jnp.sqrt(var + LN_EPS) * ln_scale
        key = jax.random.key(seed)
        ks = jax.random.split(key, 8)
        rnd = lambda k, sh, s=1.0: jax.random.normal(k, sh, dtype=jnp.float32) * s
        return {'q': rnd(ks[0], (B, S, D)), 'k': rnd(ks[1], (B, S, D)), 'v': rnd(ks[2], (B, S, D)), 'igate_w': rnd(ks[3], (NH, 3 * D), 0.02), 'igate_b': jnp.linspace(3.0, 6.0, NH, dtype=jnp.float32), 'fgate_w': rnd(ks[4], (NH, 3 * D), 0.02), 'fgate_b': rnd(ks[5], (NH,), 0.3162278), 'ln_scale': jnp.ones((D,), dtype=jnp.float32)}
    _L0_xattn_all = _L0_xattn_setup()
    _L0_xattn_in = {k: v for k, v in _L0_xattn_all.items() if k in ('igate_w', 'igate_b', 'fgate_w', 'fgate_b', 'ln_scale')}
    del _L0_xattn_all

    def _L0_ffn_setup():
        import jax, jax.numpy as jnp
        import numpy as np
        TOP_K = 2

        def _mlp(x, w1, b1, w2, b2):
            h = jax.nn.gelu(jnp.einsum('bsd,di->bsi', x, w1) + b1)
            return jnp.einsum('bsi,id->bsd', h, w2) + b2
        key = jax.random.key(seed)
        ks = jax.random.split(key, 8)
        B, S, D, I, E = (2, 256, 128, 512, 8)
        s_in = 1.0 / np.sqrt(D)
        s_mid = 1.0 / np.sqrt(I)
        return {'x': jax.random.normal(ks[0], (B, S, D), jnp.float32), 'gate_w': jax.random.normal(ks[1], (D, E), jnp.float32) * s_in, 'gate_b': jnp.zeros((E,), jnp.float32), 'sh_w1': jax.random.normal(ks[2], (D, I), jnp.float32) * s_in, 'sh_b1': jnp.zeros((I,), jnp.float32), 'sh_w2': jax.random.normal(ks[3], (I, D), jnp.float32) * s_mid, 'sh_b2': jnp.zeros((D,), jnp.float32), 'ew1': jax.random.normal(ks[4], (E, D, I), jnp.float32) * s_in, 'eb1': jnp.zeros((E, I), jnp.float32), 'ew2': jax.random.normal(ks[5], (E, I, D), jnp.float32) * s_mid, 'eb2': jnp.zeros((E, D), jnp.float32)}
    _L0_ffn_all = _L0_ffn_setup()
    _L0_ffn_in = {k: v for k, v in _L0_ffn_all.items() if k in ('gate_w', 'gate_b', 'sh_w1', 'sh_b1', 'sh_w2', 'sh_b2', 'ew1', 'eb1', 'ew2', 'eb2')}
    del _L0_ffn_all

    def _L1_attn_setup():
        import jax, jax.numpy as jnp
        import numpy as np
        DIM = 128
        NH = 16
        HD = DIM // NH
        NT = max(1, int(NH * 0.25))
        NS = NH - NT
        SCALE = HD ** (-0.5)
        key = jax.random.key(seed)
        ks = jax.random.split(key, 8)
        B, T = (2, 256)
        init = 0.02
        return {'x': jax.random.normal(ks[0], (B, T, DIM), dtype=jnp.float32), 'Wqt': jax.random.normal(ks[1], (DIM, NT * HD), dtype=jnp.float32) * init, 'Wkt': jax.random.normal(ks[2], (DIM, NT * HD), dtype=jnp.float32) * init, 'Wqs': jax.random.normal(ks[3], (DIM, NS * HD), dtype=jnp.float32) * init, 'Wks': jax.random.normal(ks[4], (DIM, NS * HD), dtype=jnp.float32) * init, 'Wv': jax.random.normal(ks[5], (DIM, DIM), dtype=jnp.float32) * init, 'Wout': jax.random.normal(ks[6], (DIM, DIM), dtype=jnp.float32) * init, 'bout': jnp.zeros((DIM,), dtype=jnp.float32), 'w_sigma': jnp.zeros((1,), dtype=jnp.float32)}
    _L1_attn_all = _L1_attn_setup()
    _L1_attn_in = {k: v for k, v in _L1_attn_all.items() if k in ('Wqt', 'Wkt', 'Wqs', 'Wks', 'Wv', 'Wout', 'bout', 'w_sigma')}
    del _L1_attn_all

    def _L1_xattn_setup():
        import jax, jax.numpy as jnp
        import numpy as np
        D1, D2, D3 = (128, 128, 128)
        key = jax.random.key(seed)
        k1, k2, kw, kb = jax.random.split(key, 4)
        x1 = jax.random.normal(k1, (8, 256, D1), dtype=jnp.float32)
        x2 = jax.random.normal(k2, (8, 256, D2), dtype=jnp.float32)
        bound = 1.0 / np.sqrt(D1 + D2)
        W = jax.random.uniform(kw, (D3, D1 + D2), minval=-bound, maxval=bound, dtype=jnp.float32)
        b = jax.random.uniform(kb, (D3,), minval=-bound, maxval=bound, dtype=jnp.float32)
        return {'x1': x1, 'x2': x2, 'W': W, 'b': b}
    _L1_xattn_all = _L1_xattn_setup()
    _L1_xattn_in = {k: v for k, v in _L1_xattn_all.items() if k in ('W', 'b')}
    del _L1_xattn_all

    def _L1_ffn_setup():
        import jax, jax.numpy as jnp
        import numpy as np
        H = 128
        I = 64
        E = 8
        K = 2
        SI = I * 2
        B, S = (2, 128)

        def _mlp(x, gw, uw, dw):
            return jax.nn.silu(x @ gw.T) * (x @ uw.T) @ dw.T
        key = jax.random.key(seed)
        ks = jax.random.split(key, 9)
        s = 0.02
        return {'x': jax.random.normal(ks[0], (B, S, H), jnp.float32), 'gate_w': jax.random.normal(ks[1], (E, H), jnp.float32) * s, 'lb_bias': jnp.zeros((E,), jnp.float32), 'expert_gate_w': jax.random.normal(ks[2], (E, I, H), jnp.float32) * s, 'expert_up_w': jax.random.normal(ks[3], (E, I, H), jnp.float32) * s, 'expert_down_w': jax.random.normal(ks[4], (E, H, I), jnp.float32) * s, 'shared_gate_w': jax.random.normal(ks[5], (SI, H), jnp.float32) * s, 'shared_up_w': jax.random.normal(ks[6], (SI, H), jnp.float32) * s, 'shared_down_w': jax.random.normal(ks[7], (H, SI), jnp.float32) * s}
    _L1_ffn_all = _L1_ffn_setup()
    _L1_ffn_in = {k: v for k, v in _L1_ffn_all.items() if k in ('gate_w', 'lb_bias', 'expert_gate_w', 'expert_up_w', 'expert_down_w', 'shared_gate_w', 'shared_up_w', 'shared_down_w')}
    del _L1_ffn_all
    return {'x': x, 'ctx_1024': ctx_1024, 'L0_attn_Wq': _L0_attn_in['Wq'], 'L0_attn_Wk': _L0_attn_in['Wk'], 'L0_attn_Wv': _L0_attn_in['Wv'], 'L0_attn_Wo': _L0_attn_in['Wo'], 'L0_attn_omega': _L0_attn_in['omega'], 'L0_attn_mu_raw': _L0_attn_in['mu_raw'], 'L0_attn_sigma_raw': _L0_attn_in['sigma_raw'], 'L0_attn_eta_raw': _L0_attn_in['eta_raw'], 'L0_attn_gamma_raw': _L0_attn_in['gamma_raw'], 'L0_attn_tau': _L0_attn_in['tau'], 'L0_attn_nu_raw': _L0_attn_in['nu_raw'], 'L0_xattn_igate_w': _L0_xattn_in['igate_w'], 'L0_xattn_igate_b': _L0_xattn_in['igate_b'], 'L0_xattn_fgate_w': _L0_xattn_in['fgate_w'], 'L0_xattn_fgate_b': _L0_xattn_in['fgate_b'], 'L0_xattn_ln_scale': _L0_xattn_in['ln_scale'], 'L0_ffn_gate_w': _L0_ffn_in['gate_w'], 'L0_ffn_gate_b': _L0_ffn_in['gate_b'], 'L0_ffn_sh_w1': _L0_ffn_in['sh_w1'], 'L0_ffn_sh_b1': _L0_ffn_in['sh_b1'], 'L0_ffn_sh_w2': _L0_ffn_in['sh_w2'], 'L0_ffn_sh_b2': _L0_ffn_in['sh_b2'], 'L0_ffn_ew1': _L0_ffn_in['ew1'], 'L0_ffn_eb1': _L0_ffn_in['eb1'], 'L0_ffn_ew2': _L0_ffn_in['ew2'], 'L0_ffn_eb2': _L0_ffn_in['eb2'], 'L1_attn_Wqt': _L1_attn_in['Wqt'], 'L1_attn_Wkt': _L1_attn_in['Wkt'], 'L1_attn_Wqs': _L1_attn_in['Wqs'], 'L1_attn_Wks': _L1_attn_in['Wks'], 'L1_attn_Wv': _L1_attn_in['Wv'], 'L1_attn_Wout': _L1_attn_in['Wout'], 'L1_attn_bout': _L1_attn_in['bout'], 'L1_attn_w_sigma': _L1_attn_in['w_sigma'], 'L1_xattn_W': _L1_xattn_in['W'], 'L1_xattn_b': _L1_xattn_in['b'], 'L1_ffn_gate_w': _L1_ffn_in['gate_w'], 'L1_ffn_lb_bias': _L1_ffn_in['lb_bias'], 'L1_ffn_expert_gate_w': _L1_ffn_in['expert_gate_w'], 'L1_ffn_expert_up_w': _L1_ffn_in['expert_up_w'], 'L1_ffn_expert_down_w': _L1_ffn_in['expert_down_w'], 'L1_ffn_shared_gate_w': _L1_ffn_in['shared_gate_w'], 'L1_ffn_shared_up_w': _L1_ffn_in['shared_up_w'], 'L1_ffn_shared_down_w': _L1_ffn_in['shared_down_w']}

def reference(x, ctx_1024, L0_attn_Wq, L0_attn_Wk, L0_attn_Wv, L0_attn_Wo, L0_attn_omega, L0_attn_mu_raw, L0_attn_sigma_raw, L0_attn_eta_raw, L0_attn_gamma_raw, L0_attn_tau, L0_attn_nu_raw, L0_xattn_igate_w, L0_xattn_igate_b, L0_xattn_fgate_w, L0_xattn_fgate_b, L0_xattn_ln_scale, L0_ffn_gate_w, L0_ffn_gate_b, L0_ffn_sh_w1, L0_ffn_sh_b1, L0_ffn_sh_w2, L0_ffn_sh_b2, L0_ffn_ew1, L0_ffn_eb1, L0_ffn_ew2, L0_ffn_eb2, L1_attn_Wqt, L1_attn_Wkt, L1_attn_Wqs, L1_attn_Wks, L1_attn_Wv, L1_attn_Wout, L1_attn_bout, L1_attn_w_sigma, L1_xattn_W, L1_xattn_b, L1_ffn_gate_w, L1_ffn_lb_bias, L1_ffn_expert_gate_w, L1_ffn_expert_up_w, L1_ffn_expert_down_w, L1_ffn_shared_gate_w, L1_ffn_shared_up_w, L1_ffn_shared_down_w):
    import jax
    import jax.numpy as jnp

    def _L0_attn_ref(x, Wq, Wk, Wv, Wo, omega, mu_raw, sigma_raw, eta_raw, gamma_raw, tau, nu_raw):
        import jax, jax.numpy as jnp
        import numpy as np
        B, N, DE, H, DH = (2, 128, 128, 16, 64)
        DK = H * DH
        MIN_EXP = -30.0
        EPS = 0.0001
        B_, N_, _ = x.shape
        H_, d_half = omega.shape
        DH_ = 2 * d_half
        DKt = H_ * DH_

        def cproj(W):
            z = x @ W
            D = W.shape[1] // 2
            zc = jax.lax.complex(z[..., :D], z[..., D:])
            return zc.reshape(B_, N_, H_, DH_)
        q, k, v = (cproj(Wq), cproj(Wk), cproj(Wv))
        om = jnp.concatenate([omega, -omega], axis=-1)
        t = jnp.arange(N_, dtype=jnp.float32)
        ang = t[:, None, None] * om[None]
        phase = jax.lax.complex(jnp.cos(ang), jnp.sin(ang))
        qr = q * phase[None]
        kr = k * phase[None]
        mu = jax.nn.sigmoid(mu_raw) + EPS
        dt = jnp.abs(t[:, None] - t[None, :])
        E = jnp.exp(jnp.clip(-mu[:, None, None] * dt[None], MIN_EXP, 0.0))
        s = jnp.einsum('bihd,bjhd->bhij', qr, jnp.conj(kr)).real
        qn = (q.real ** 2 + q.imag ** 2).sum(-1).transpose(0, 2, 1)
        kn = (k.real ** 2 + k.imag ** 2).sum(-1).transpose(0, 2, 1)
        sigma_sq = jax.nn.softplus(sigma_raw)
        eta_sq = jax.nn.softplus(eta_raw)
        gamma_sq = jax.nn.softplus(gamma_raw)
        V = (sigma_sq / (2.0 * mu))[:, None, None] * (1.0 - E * E) + (eta_sq + gamma_sq)[:, None, None]
        maha = jnp.maximum(qn[..., None] + (E * E)[None] * kn[:, :, None, :] - 2.0 * E[None] * s, 0.0) / V[None]
        nu = jax.nn.softplus(nu_raw)
        coef = (-0.5 * tau * (nu + DH_))[None, :, None, None]
        logits = coef * jnp.log1p(maha / nu[None, :, None, None]) - 0.5 * DH_ * jnp.log(V)[None]
        causal = t[:, None] >= t[None, :]
        logits = jnp.where(causal[None, None], logits, -jnp.inf)
        A = jax.nn.softmax(logits, axis=-1)
        out = jnp.einsum('bhij,bjhd->bihd', A.astype(v.dtype), v)
        y = jnp.concatenate([out.real.reshape(B_, N_, DKt), out.imag.reshape(B_, N_, DKt)], axis=-1)
        return y @ Wo

    def _L0_xattn_ref(q, k, v, igate_w, igate_b, fgate_w, fgate_b, ln_scale):
        import jax, jax.numpy as jnp
        import numpy as np
        B, S, D, NH = (2, 256, 128, 8)
        DH = D // NH
        EPS = 1e-06
        LN_EPS = 1e-05

        def _mlstm_cell(q, k, v, igate_w, igate_b, fgate_w, fgate_b, ln_scale):
            Slen = q.shape[0]
            ifg = jnp.concatenate([q, k, v], axis=-1)
            ig = (ifg @ igate_w.T + igate_b).T
            fg = (ifg @ fgate_w.T + fgate_b).T
            qh = q.reshape(Slen, NH, DH).transpose(1, 0, 2)
            kh = k.reshape(Slen, NH, DH).transpose(1, 0, 2)
            vh = v.reshape(Slen, NH, DH).transpose(1, 0, 2)
            log_f = jax.nn.log_sigmoid(fg)
            cs = jnp.cumsum(log_f, axis=1)
            fg_mat = cs[:, :, None] - cs[:, None, :]
            mask = jnp.tril(jnp.ones((Slen, Slen), dtype=bool))
            log_fg_mat = jnp.where(mask, fg_mat, -jnp.inf)
            log_D = log_fg_mat + ig[:, None, :]
            max_log_D = jnp.max(log_D, axis=-1, keepdims=True)
            D_mat = jnp.exp(log_D - max_log_D)
            qk = jnp.einsum('hsd,htd->hst', qh, kh) / np.sqrt(DH)
            C = qk * D_mat
            normalizer = jnp.maximum(jnp.abs(C.sum(axis=-1, keepdims=True)), jnp.exp(-max_log_D))
            h = jnp.einsum('hst,htd->hsd', C / (normalizer + EPS), vh)
            h = h.transpose(1, 0, 2).reshape(Slen, D)
            mu = h.mean(axis=-1, keepdims=True)
            var = h.var(axis=-1, keepdims=True)
            return (h - mu) / jnp.sqrt(var + LN_EPS) * ln_scale
        return jax.vmap(lambda qq, kk, vv: _mlstm_cell(qq, kk, vv, igate_w, igate_b, fgate_w, fgate_b, ln_scale))(q, k, v)

    def _L0_ffn_ref(x, gate_w, gate_b, sh_w1, sh_b1, sh_w2, sh_b2, ew1, eb1, ew2, eb2):
        import jax, jax.numpy as jnp
        import numpy as np
        TOP_K = 2

        def _mlp(x, w1, b1, w2, b2):
            h = jax.nn.gelu(jnp.einsum('bsd,di->bsi', x, w1) + b1)
            return jnp.einsum('bsi,id->bsd', h, w2) + b2
        E = ew1.shape[0]
        router_probs = jax.nn.softmax(jnp.einsum('bsd,de->bse', x, gate_w) + gate_b, axis=-1)
        expert_values, expert_indices = jax.lax.top_k(router_probs, k=TOP_K)
        expert_values = expert_values / (jnp.sum(expert_values, axis=-1, keepdims=True) + 1e-09)
        h = jax.nn.gelu(jnp.einsum('bsd,edi->bsei', x, ew1) + eb1)
        all_outputs = jnp.einsum('bsei,eid->bsed', h, ew2) + eb2
        one_hot = jax.nn.one_hot(expert_indices, E, dtype=x.dtype)
        weights_E = (one_hot * expert_values[..., None]).sum(axis=2)
        moe_out = jnp.einsum('bse,bsed->bsd', weights_E, all_outputs)
        return x + _mlp(x, sh_w1, sh_b1, sh_w2, sh_b2) + moe_out

    def _L1_attn_ref(x, Wqt, Wkt, Wqs, Wks, Wv, Wout, bout, w_sigma):
        import jax, jax.numpy as jnp
        import numpy as np
        DIM = 128
        NH = 16
        HD = DIM // NH
        NT = max(1, int(NH * 0.25))
        NS = NH - NT
        SCALE = HD ** (-0.5)
        B, T, D = x.shape
        Qt = (x @ Wqt).reshape(B, T, NT, HD)
        Kt = (x @ Wkt).reshape(B, T, NT, HD)
        Qs = (x @ Wqs).reshape(B, T, NS, HD)
        Ks = (x @ Wks).reshape(B, T, NS, HD)
        st = jnp.einsum('bthd,bshd->bths', Qt, Kt)
        ss = jnp.einsum('bthd,bshd->bths', Qs, Ks)
        sig = jax.nn.sigmoid(w_sigma)
        score = jnp.concatenate([-sig * st, ss], axis=2) * SCALE
        attn = jax.nn.softmax(score, axis=-1)
        V = (x @ Wv).reshape(B, T, NH, HD)
        ctx = jnp.einsum('bths,bshd->bthd', attn, V).reshape(B, T, D)
        return ctx @ Wout + bout

    def _L1_xattn_ref(x1, x2, W, b):
        import jax, jax.numpy as jnp
        import numpy as np
        D1, D2, D3 = (128, 128, 128)
        d1 = x1.shape[-1]
        W1 = W[:, :d1]
        W2 = W[:, d1:]
        part1 = jnp.einsum('bld,ed->ble', x1, W1)
        part2 = jnp.einsum('bld,ed->be', x2, W2) / x2.shape[1]
        return part1 + part2[:, None, :] + b

    def _L1_ffn_ref(x, gate_w, lb_bias, expert_gate_w, expert_up_w, expert_down_w, shared_gate_w, shared_up_w, shared_down_w):
        import jax, jax.numpy as jnp
        import numpy as np
        H = 128
        I = 64
        E = 8
        K = 2
        SI = I * 2
        B, S = (2, 128)

        def _mlp(x, gw, uw, dw):
            return jax.nn.silu(x @ gw.T) * (x @ uw.T) @ dw.T
        b, s, h = x.shape
        xf = x.reshape(-1, h)
        logits = xf @ gate_w.T + lb_bias
        scores = jax.nn.sigmoid(logits.astype(jnp.float32))
        topw, topi = jax.lax.top_k(scores, K)
        topw = (topw / (topw.sum(-1, keepdims=True) + 1e-08)).astype(x.dtype)
        out = jnp.zeros_like(xf)
        for e in range(E):
            m = topi == e
            sel = m.any(axis=-1)
            cnt = m.sum()
            wmean = (topw * m).sum() / jnp.maximum(cnt, 1).astype(topw.dtype)
            y = _mlp(xf, expert_gate_w[e], expert_up_w[e], expert_down_w[e])
            out = out + jnp.where(sel[:, None], y * wmean, jnp.zeros((), x.dtype))
        out = out.reshape(b, s, h)
        out = out + _mlp(x, shared_gate_w, shared_up_w, shared_down_w)
        return out
    x = _layernorm(x + _L0_attn_ref(x, L0_attn_Wq, L0_attn_Wk, L0_attn_Wv, L0_attn_Wo, L0_attn_omega, L0_attn_mu_raw, L0_attn_sigma_raw, L0_attn_eta_raw, L0_attn_gamma_raw, L0_attn_tau, L0_attn_nu_raw), axis=-1)
    x = _layernorm(x + _L0_xattn_ref(x, ctx_1024, ctx_1024, L0_xattn_igate_w, L0_xattn_igate_b, L0_xattn_fgate_w, L0_xattn_fgate_b, L0_xattn_ln_scale), axis=-1)
    x = _layernorm(x + _L0_ffn_ref(x, L0_ffn_gate_w, L0_ffn_gate_b, L0_ffn_sh_w1, L0_ffn_sh_b1, L0_ffn_sh_w2, L0_ffn_sh_b2, L0_ffn_ew1, L0_ffn_eb1, L0_ffn_ew2, L0_ffn_eb2), axis=-1)
    x = _layernorm(x + _L1_attn_ref(x, L1_attn_Wqt, L1_attn_Wkt, L1_attn_Wqs, L1_attn_Wks, L1_attn_Wv, L1_attn_Wout, L1_attn_bout, L1_attn_w_sigma), axis=-1)
    x = _layernorm(x + _L1_xattn_ref(x, ctx_1024, L1_xattn_W, L1_xattn_b), axis=-1)
    x = _layernorm(x + _L1_ffn_ref(x, L1_ffn_gate_w, L1_ffn_lb_bias, L1_ffn_expert_gate_w, L1_ffn_expert_up_w, L1_ffn_expert_down_w, L1_ffn_shared_gate_w, L1_ffn_shared_up_w, L1_ffn_shared_down_w), axis=-1)
    return x

_drawn_inputs = setup_inputs


def setup_inputs(seed=0):
    import zlib

    import numpy as np

    out = dict(_drawn_inputs(seed))
    spreads = {'L0_attn_eta_raw': (1.0, 0.6),
     'L0_attn_gamma_raw': (1.0, 0.6),
     'L0_attn_tau': (1.0, 0.2),
     'L0_attn_nu_raw': (4.0, 0.2),
     'L0_xattn_ln_scale': (1.0, 0.2),
     'L0_ffn_gate_b': (0.0, 0.1),
     'L0_ffn_sh_b1': (0.0, 0.1),
     'L0_ffn_sh_b2': (0.0, 0.1),
     'L0_ffn_eb1': (0.0, 0.354),
     'L0_ffn_eb2': (0.0, 0.1),
     'L1_attn_bout': (0.0, 0.1),
     'L1_ffn_lb_bias': (0.0, 0.8)}
    factors = {'L1_attn_Wqt': 8.0,
     'L1_attn_Wkt': 8.0,
     'L1_attn_Wqs': 8.0,
     'L1_attn_Wks': 8.0,
     'L1_attn_Wv': 5.367,
     'L1_attn_Wout': 5.474,
     'L1_ffn_gate_w': 8.0,
     'L1_ffn_expert_gate_w': 8.0,
     'L1_ffn_expert_up_w': 8.0,
     'L1_ffn_expert_down_w': 8.0,
     'L1_ffn_shared_gate_w': 8.0,
     'L1_ffn_shared_up_w': 8.0,
     'L1_ffn_shared_down_w': 8.0}
    for name, (base, spread) in spreads.items():
        noise = np.random.default_rng([zlib.crc32(name.encode()), seed]).standard_normal(out[name].shape)
        drawn = base * np.exp(spread * noise) if base else spread * noise
        out[name] = jnp.asarray(drawn.astype(out[name].dtype))
    for name, factor in factors.items():
        out[name] = (out[name] * factor).astype(out[name].dtype)
    return out
```

```python
import math
from contextlib import ExitStack

import concourse.bass as bass
from concourse import mybir

B, N, D = 32, 128, 128
GB = 4
G = B // GB
W = GB * N
H0, DH0 = 16, 64
H1, DH1 = 8, 16
E0, I0 = 8, 512
CH = I0 // 128
E0S = E0 + 1
H2, DH2 = 16, 8
H2T = H2 // 4
E1, I1 = 8, 64
PAIRS = E1 * I1 // 128
BLK = PAIRS + 1
NEG = -1.0e30
LNS = 6


def decoder(nc, a, out, x5_scratch, x5T_scratch):
    fp32, bf16 = mybir.dt.float32, mybir.dt.bfloat16
    ALU = mybir.AluOpType
    ACT = mybir.ActivationFunctionType
    X = mybir.AxisListType.X

    with ExitStack() as ctx:
        def sb(name, *shape, dtype=fp32):
            return ctx.enter_context(nc.sbuf_tensor(name, list(shape), dtype))

        def sem(name):
            return ctx.enter_context(nc.semaphore(name))

        bank = [ctx.enter_context(nc.psum_tensor(f"bank{i}", [128, W], fp32)) for i in range(8)]

        def rows(ap, d=D):
            return ap[:, 0:GB * d].rearrange("p (b d) -> p b d", b=GB)

        work = sb("work", 128, 24 * W)
        wk = [work[:, i * W:(i + 1) * W] for i in range(24)]
        streamed = ("x_row", "x_T", "ctx_row", "ctx_T")
        phase2 = ("w_g1", "w_u1", "w_d1", "sel2")
        res = {name: sb("sb_" + name, *a[name].shape) for name in a
               if name not in streamed + phase2 + ("dist", "tramp", "wvT0", "wo0", "sel24")}
        res["dist"], res["tramp"] = wk[0][:, 0:N], wk[0][:, N:2 * N]
        res["sel24"] = work[0:72, 2 * W:4 * W].rearrange("p (h n) -> p h n", h=H1)
        sel24, m_parts = sb("sel24", 72, H1, 128, dtype=bf16), sb("m_parts", 72, W, dtype=bf16)
        res["wvT0"], res["wo0"] = (work[:, i * W:(i + 4) * W].rearrange("p (h d) -> p h d", h=H0) for i in (4, 8))
        for_tables = ("par", "cols", "tramp", "freq", "dist", "mask_ij")
        rest = [name for name in res if name not in for_tables]
        late, at = {}, 10 * W
        for name in phase2:
            shape = a[name].shape
            size = shape[1] * shape[2]
            late[name] = work[0:shape[0], at:at + size].rearrange("p (k n) -> p k n", k=shape[1])
            at += size
        ident, dist, mask_ij, mask_ji, tramp, cols = (res[k] for k in
                                                      ("ident", "dist", "mask_ij", "mask_ji", "tramp", "cols"))
        sgn, top_rows, low_rows, ones_col, half_col = (cols[:, i:i + 1] for i in range(5))
        head_mask1 = cols[:, 8:16]
        head_mask2 = cols[:, 16:32]
        rank = cols[:, 32:40]

        cosT, sinT, dec, dec_inv, wgt, bias_t = (sb(n, 128, H0, N) for n in
                                                 ("cosT", "sinT", "dec", "dec_inv", "wgt", "bias_t"))
        vo = sb("vo", 128, H0, D)
        par = res["par"]
        p_abs = sb("p_abs", 128, 4 * H0)
        p_sp = sb("p_sp", 128, 4 * H0)
        p_sig = sb("p_sig", 128, H0 + 1)
        p_col = sb("p_col", 128, 7, H0)
        q_scale = sb("q_scale", 128, 1)

        x_row, x_T, ctx_T = sb("x_row", 128, GB, D), sb("x_T", 128, W), sb("ctx_T", 128, W)
        v1 = sb("v1", 128, GB, H1, DH1 + 1)
        act_row = [sb(f"act_row{i}", 128, GB, D) for i in range(2)]
        act_T = sb("act_T", 128, W)
        resid = rows(wk[21])
        st, mv = sb("st", 128, GB, 6), sb("mv", 128, GB, 2)
        ln_t, rstd = sb("ln_t", 128, GB), sb("rstd", 128, GB)

        nrm = sb("nrm", 128, 2, 8)
        negmax = sb("negmax", 128, 2, GB)
        esum = sb("esum", 128, 4, GB)
        rsum = sb("rsum", 128, 2, GB)

        gate = [wk[6 + i][0:8, :] for i in range(6)] + [sb("gate_ones", 8, W)]
        aT, eM = sb("aT", 128, GB, H1), sb("eM", 128, GB, H1)
        den, rden = sb("den", 128, GB, H1), sb("rden", 128, GB, H1)
        rt = [sb(f"rt{i}", 128, GB, E0) for i in range(6)]
        r1 = [sb(f"r1{i}", 128, GB) for i in range(6)]
        wexp, wexpT = sb("wexp", 128, GB, E0), wk[9][0:8, :]
        v2 = sb("v2", 128, GB, H2, DH2 + 1)
        den2 = sb("den2", 128, GB, H2)
        csum, cbc = sb("csum", 128, GB), rows(wk[11])
        sel = sb("sel", 128, GB, E1)
        logit1, sel1 = sb("logit1", 128, G, GB, E1), sb("sel1", 128, G, GB, E1)
        router_sum = sb("router_sum", 128, 2, E1)
        wmean = sb("wmean", 8, 4)
        selT = wk[7][0:8, :]

        loaded, loaded_first, tables, par_a, par_v = (sem(n) for n in (
            "loaded", "loaded_first", "tables", "par_a", "par_v"))
        in_x, in_ctx = sem("in_x"), sem("in_ctx")
        chain_v, chain_a = sem("chain_v"), sem("chain_a")
        q_proj, k_proj, v_proj = sem("q_proj"), sem("k_proj"), sem("v_proj")
        q_parts, k_parts, qk_rot = sem("q_parts"), sem("k_parts"), sem("qk_rot")
        squares, norms, norms_sb, diag_done = sem("squares"), sem("norms"), sem("norms_sb"), sem("diag_done")
        v_sb, score, maha, log_done = sem("v_sb"), sem("score"), sem("maha"), sem("log_done")
        logits, exped, prob, prob_T, prob_T_sb = (sem(n) for n in
                                                  ("logits", "exped", "prob", "prob_T", "prob_T_sb"))
        fold, fold_sb, sums_inv, head_out = (sem(n) for n in ("fold", "fold_sb", "sums_inv", "head_out"))
        ln_stats, ln_rstd, ln_out, act_tr, act_T_sb = (sem(n) for n in
                                                       ("ln_stats", "ln_rstd", "ln_out", "act_tr", "act_T_sb"))
        gates, gate_v, gate_a, gate_rows, gate_T, gate_aT, gate_eM = (sem(n) for n in (
            "gates", "gate_v", "gate_a", "gate_rows", "gate_T", "gate_aT", "gate_eM"))
        gate_max, gate_tot = sem("gate_max"), sem("gate_tot")
        mx_bc, arg_done, dmat, ctx_masked, qk1, c_done, num = (sem(n) for n in (
            "mx_bc", "arg_done", "dmat", "ctx_masked", "qk1", "c_done", "num"))
        rt_logit, rt_v, rt_a, rt_w, rt_wT, rt_wT_sb, rt_bias, xb_done = (sem(n) for n in (
            "rt_logit", "rt_v", "rt_a", "rt_w", "rt_wT", "rt_wT_sb", "rt_bias", "xb_done"))
        up, gelu, down, moe_acc = sem("up"), sem("gelu"), sem("down"), sem("moe_acc")
        qkv2, q2_sb, kv2_sb, k2_masked, s2, z2, p2, pT2, pT2_sb, o2 = (sem(n) for n in (
            "qkv2", "q2_sb", "kv2_sb", "k2_masked", "s2", "z2", "p2", "pT2", "pT2_sb", "o2"))
        o2_row, o2_tr, o2_T, y2, y3, ctx_mean = (sem(n) for n in ("o2_row", "o2_tr", "o2_T", "y2", "y3", "ctx_mean"))
        rl_logit, rl_v, rl_a, stored = (sem(n) for n in ("rl_logit", "rl_v", "rl_a", "stored"))
        sel_here = sem("sel_here")
        tot, sums_done, in2, selT_ps, selT_sb = (sem(n) for n in ("tot", "sums_done", "in2", "selT_ps", "selT_sb"))
        gup, silu, h_done, y4, f_stats, f_rstd, f_out, out_done = (sem(n) for n in (
            "gup", "silu", "h_done", "y4", "f_stats", "f_rstd", "f_out", "out_done"))

        block = ctx.enter_context(nc.Block())

        @block.sync
        def _(sp):
            for name in for_tables:
                sp.dma_start(res[name][:], a[name]).then_inc(loaded_first, 16)
            for name in rest:
                sp.dma_start(res[name][:], a[name]).then_inc(loaded, 16)
            sp.sem_inc(stored, 16)
            sp.sem_inc(out_done, 16)
            with sp.Fori(0, G) as g:
                def src(name):
                    v = a[name]
                    return v[bass.ds(g, 1)].rearrange("g p n -> (g p) n")
                sp.wait_ge(stored, g * 32 + 16)
                sp.wait_ge(ln_out, g * LNS + 1)
                sp.dma_start(ctx_T[:], src("ctx_T")).then_inc(in_ctx, 16)
                sp.dma_start(wk[23][:], src("ctx_row")).then_inc(in_ctx, 16)
                sp.wait_ge(act_T_sb, g * 5 + 5)
                sp.dma_start(x5_scratch[bass.ds(g, 1)].rearrange("g p n -> (g p) n"),
                             act_row[0][:].rearrange("p b d -> p (b d)")).then_inc(stored, 16)
                sp.dma_start(x5T_scratch[bass.ds(g, 1)].rearrange("g p n -> (g p) n"),
                             act_T[:]).then_inc(stored, 16)
            sp.wait_ge(stored, G * 32 + 16)
            sp.wait_ge(f_out, 1)
            for name in phase2:
                sp.dma_start(late[name], a[name]).then_inc(in2, 16)
            with sp.Fori(0, G) as g:
                sp.wait_ge(f_out, g + 1)
                sp.wait_ge(out_done, g * 16 + 16)
                sp.dma_start(x_row[:].rearrange("p b d -> p (b d)"),
                             x5_scratch[bass.ds(g, 1)].rearrange("g p n -> (g p) n")).then_inc(in2, 16)
                sp.dma_start(x_T[:], x5T_scratch[bass.ds(g, 1)].rearrange("g p n -> (g p) n")).then_inc(in2, 16)
                sp.wait_ge(f_out, g + 2)
                sp.dma_start(out[bass.ds(g, 1)].rearrange("g b t d -> t (g b) d"),
                             act_row[0][:]).then_inc(out_done, 16)
            sp.wait_ge(out_done, 16 * G + 16)

        @block.vector
        def _(dve):
            v = nc.vector
            count = [0]

            def link(ins):
                count[0] += 1
                ins.then_inc(chain_v, 1)
                dve.wait_ge(chain_v, count[0])

            def restart():
                dve.sem_clear(chain_v)
                count[0] = 0

            restart()
            dve.wait_ge(loaded_first, 16 * len(for_tables))

            v.scalar_tensor_tensor(p_abs[:], par[:, 0:64], -1.0, par[:, 0:64], ALU.mult, ALU.min).then_inc(par_v, 1)
            dve.wait_ge(par_a, 1)
            link(v.scalar_tensor_tensor(p_sp[:], par[:, 0:64], 0.0, p_abs[:], ALU.max, ALU.add))
            dve.wait_ge(par_a, 2)
            link(v.tensor_scalar(p_sig[:], p_sig[:], 1.0, None, ALU.add))
            link(v.reciprocal(p_sig[:], p_sig[:]))
            sig, eta, gam, nu = (p_sp[:, 16 * i:16 * i + 16] for i in range(4))
            tau = par[:, 64:80]
            mu = p_sig[:, 0:H0]
            neg_mu, coef, amp, neg_amp, base, rmu, rnu = (p_col[:, i, :] for i in range(7))
            link(v.tensor_scalar(mu, mu, 1.0e-4, None, ALU.add))
            v.tensor_scalar(neg_mu, mu, -1.0, None, ALU.mult)
            link(v.reciprocal(rmu, mu))
            link(v.scalar_tensor_tensor(amp, sig, 0.5, rmu, ALU.mult, ALU.mult))
            v.tensor_scalar(neg_amp, amp, -1.0, None, ALU.mult)
            link(v.tensor_tensor(base, eta, gam, ALU.add))
            link(v.tensor_tensor(base, base, amp, ALU.add))
            link(v.scalar_tensor_tensor(coef, nu, float(DH0), tau, ALU.add, ALU.mult))
            link(v.tensor_scalar(coef, coef, -0.5, None, ALU.mult))
            sc = DH2 ** -0.5
            link(v.tensor_scalar(q_scale[:], p_sig[:, H0:H0 + 1], -sc, None, ALU.mult))
            link(v.tensor_tensor(q_scale[:], q_scale[:], top_rows, ALU.mult))
            link(v.scalar_tensor_tensor(q_scale[:], low_rows, sc, q_scale[:], ALU.mult, ALU.add))

            MAGIC, C1, C2 = 12582912.0, 6.28125, 0.0019350051879882812
            C3 = 2 * math.pi - C1 - C2
            PI = 3.1415925
            ang, turns, red = dec, dec_inv, wgt
            for h in range(H0):
                last = v.tensor_scalar(ang[:, h], tramp[:], res["freq"][:, h:h + 1], None, ALU.mult)
            link(last)
            link(v.tensor_scalar(turns[:], ang[:], 1 / (2 * math.pi), MAGIC, ALU.mult, ALU.add))
            link(v.tensor_scalar(turns[:], turns[:], -MAGIC, None, ALU.add))
            link(v.scalar_tensor_tensor(red[:], turns[:], -C1, ang[:], ALU.mult, ALU.add))
            link(v.scalar_tensor_tensor(red[:], turns[:], -C2, red[:], ALU.mult, ALU.add))
            link(v.scalar_tensor_tensor(red[:], turns[:], -C3, red[:], ALU.mult, ALU.add))
            link(v.tensor_scalar(red[:], red[:], PI, -PI, ALU.min, ALU.max))
            v.tensor_scalar(turns[:], red[:], math.pi / 2, -2 * math.pi, ALU.is_gt, ALU.mult).then_inc(par_v, 1)
            dve.wait_ge(par_v, 2)
            link(v.scalar_tensor_tensor(turns[:], red[:], math.pi / 2, turns[:], ALU.add, ALU.add))
            v.tensor_scalar(turns[:], turns[:], PI, -PI, ALU.min, ALU.max).then_inc(par_v, 1)
            dve.wait_ge(par_a, 4)
            link(v.tensor_scalar(sinT[:], sinT[:], sgn, None, ALU.mult))

            for h in range(H0):
                last = v.tensor_scalar(dec[:, h], dist[:], neg_mu[:, h:h + 1], -30.0, ALU.mult, ALU.max)
            last.then_inc(par_v, 1)
            dve.wait_ge(par_a, 5)
            link(v.tensor_tensor(bias_t[:], dec[:], dec_inv[:], ALU.mult))
            link(v.tensor_scalar(bias_t[:], bias_t[:], -1.0, 2.0, ALU.mult, ALU.add))
            link(v.tensor_tensor(dec_inv[:], dec_inv[:], bias_t[:], ALU.mult))
            link(v.tensor_tensor(bias_t[:], dec[:], dec[:], ALU.mult))
            for h in range(H0):
                last = v.tensor_scalar(bias_t[:, h], bias_t[:, h], neg_amp[:, h:h + 1], base[:, h:h + 1],
                                       ALU.mult, ALU.add)
            last.then_inc(par_v, 1)
            link(v.reciprocal(rnu, nu))
            link(v.tensor_scalar(rnu, rnu, -2.0, None, ALU.mult))
            v.memset(v1[:], 1.0)
            v.memset(m_parts[:], 0.0)
            dve.wait_ge(par_a, 6)
            for h in range(H0):
                last = v.scalar_tensor_tensor(wgt[:, h], dec[:, h], rnu[:, h:h + 1], wgt[:, h], ALU.mult, ALU.mult)
            link(last)
            mask_b = mask_ij[:].unsqueeze(1).broadcast_to([128, H0, N])
            dve.wait_ge(loaded, 16 * len(rest))
            v.tensor_copy(sel24[:], res["sel24"])
            v.tensor_tensor(res["gate_w"][:, 1], res["gate_w"][:, 1], res["gate_w"][:, 2], ALU.add)
            v.memset(v2[:], 1.0)
            v.memset(gate[6][:], 1.0).then_inc(ln_out, 1)
            v.scalar_tensor_tensor(bias_t[:], bias_t[:], -0.5 * DH0, mask_b, ALU.mult, ALU.add).then_inc(tables, 1)
            dve.wait_ge(tables, 1)

            def norm(g, i, src, dst, stats=ln_stats, rs=ln_rstd, per=LNS, done=None):
                for b in range(GB):
                    last = v.bn_stats(st[:, b, :], src[:, b])
                link(last)
                for b in range(GB):
                    last = v.bn_aggr(mv[:, b, :], st[:, b, :])
                last.then_inc(stats, 1)
                dve.wait_ge(rs, g * per + i + 1)
                for b in range(GB):
                    last = v.tensor_scalar(dst[:, b], src[:, b], mv[:, b, 0:1], rstd[:, b:b + 1],
                                           ALU.subtract, ALU.mult)
                last.then_inc(done, 1)

            def bc(m):
                return m.unsqueeze(2).broadcast_to([128, m.shape[1], 8])

            def top2(p, oh1, oh2, m1, m2, t, r):
                rk = rank.unsqueeze(1).broadcast_to([128, m1.shape[1], 8])
                for oh, m in ((oh1, m1), (oh2, m2)):
                    q = p if oh is oh1 else t
                    link(v.tensor_reduce(m, q, X, ALU.max))
                    link(v.tensor_tensor(oh, q, bc(m), ALU.is_equal))
                    link(v.tensor_tensor(oh, oh, rk, ALU.mult))
                    link(v.tensor_reduce(r, oh, X, ALU.max))
                    link(v.tensor_tensor(oh, rk, bc(r), ALU.is_equal))
                    if oh is oh1:
                        link(v.scalar_tensor_tensor(t, oh, -4.0, p, ALU.mult, ALU.add))

            with dve.Fori(0, G) as g:
                restart()
                bc_h = lambda t, h: t[:, h].unsqueeze(1).broadcast_to([128, GB, N])
                half = ((slice(0, DH0), slice(DH0, 128)), (slice(DH0, 128), slice(0, DH0)))
                for s in range(H0 + 5):
                    h = s - 5
                    if 0 <= h < H0:
                        dve.wait_ge(exped, g * H0 + h + 1)
                        if h >= 2:
                            dve.wait_ge(prob, g * H0 + h - 1)
                        v.reciprocal(rsum[:, h % 2, :], esum[:, h % 4, :]).then_inc(sums_inv, 1)
                    if s < H0:
                        if s > 0:
                            dve.wait_ge(qk_rot, g * 2 * H0 + 2 * s)
                        for i, sm, dn in ((0, q_proj, q_parts), (2, k_proj, k_parts)):
                            src = bank[i // 2]
                            dve.wait_ge(sm, g * H0 + s + 1)
                            v.tensor_tensor(rows(wk[i]), rows(src), bc_h(cosT, s), ALU.mult)
                            for o, p in half:
                                last = v.tensor_tensor(rows(wk[i + 1][o]), rows(src[p]),
                                                       sinT[o, s].unsqueeze(1).broadcast_to([DH0, GB, N]), ALU.mult)
                            last.then_inc(dn, 1)
                    h = s - 2
                    if 0 <= h < H0:
                        M = rows(wk[(11, 21)[h % 2]])
                        dve.wait_ge(norms_sb, g * H0 + h + 1)
                        dve.wait_ge(score, g * H0 + h + 1)
                        for b in range(GB):
                            last = v.scalar_tensor_tensor(M[:, b], dec_inv[:, h], nrm[:, h % 2, 4 + b:5 + b],
                                                          rows(bank[4 + h % 2])[:, b], ALU.mult, ALU.add)
                        link(last)
                        v.scalar_tensor_tensor(M, M, 0.0, bc_h(wgt, h), ALU.min, ALU.mult).then_inc(maha, 1)
                    h = s - 3
                    if 0 <= h < H0:
                        dve.wait_ge(log_done, g * H0 + h + 1)
                        if h > 0:
                            dve.wait_ge(exped, g * H0 + h)
                        link(v.scalar_tensor_tensor(rows(wk[12]), rows(wk[(11, 21)[h % 2]]), coef[:, h:h + 1],
                                                    bc_h(bias_t, h), ALU.mult, ALU.add))
                        v.tensor_reduce(negmax[:, h % 2, :], rows(wk[12]), X, ALU.max,
                                        negate=True).then_inc(logits, 1)
                dve.wait_ge(head_out, g * H0 + H0)
                link(v.tensor_tensor(resid, rows(bank[7]), x_row[:], ALU.add))
                dve.wait_ge(in_ctx, g * 32 + 32)
                norm(g, 0, resid, act_row[0], done=ln_out)

                nabs, e_g, logf, csum_f, a_g, m_g, one = gate
                b_i, b_f = res["gate_b"][0:8, :], res["gate_b"][32:40, :]
                v.tensor_copy(v1[:, :, :, 0:DH1], wk[23][:].rearrange("p (b h d) -> p b h d", b=GB, h=H1))
                dve.wait_ge(gates, g + 1)
                link(v.tensor_scalar(logf[:], bank[0][32:40, :], b_f, None, ALU.add))
                v.scalar_tensor_tensor(nabs[:], logf[:], -1.0, logf[:], ALU.mult, ALU.min).then_inc(gate_v, 1)
                dve.wait_ge(gate_a, g + 1)
                link(v.scalar_tensor_tensor(logf[:], logf[:], 0.0, e_g[:], ALU.min, ALU.subtract))
                for b in range(GB):
                    c = slice(b * N, b * N + N)
                    last = v.tensor_tensor_scan(csum_f[:, c], one[:, c], logf[:, c], 0.0, ALU.mult, ALU.add)
                link(last)
                v.scalar_tensor_tensor(a_g[:], bank[0][0:8, :], b_i, csum_f[:], ALU.add,
                                       ALU.subtract).then_inc(gate_rows, 1)
                dve.wait_ge(gate_rows, g + 1)
                for b in range(GB):
                    c = slice(b * N, b * N + N)
                    last = v.tensor_tensor_scan(m_g[:, c], one[:, c], a_g[:, c], -3.0e38, ALU.mult, ALU.max)
                link(last)
                link(v.tensor_copy(m_parts[0:8, :], m_g[:]))
                link(v.tensor_tensor(logf[:], m_g[:], m_parts[0:8, :], ALU.subtract))
                link(v.tensor_copy(m_parts[32:40, :], logf[:]))
                v.tensor_tensor(m_parts[64:72, :], logf[:], m_parts[32:40, :], ALU.subtract).then_inc(gate_max, 1)
                v.tensor_tensor(csum_f[:], csum_f[:], m_g[:], ALU.add).then_inc(gate_tot, 1)
                dve.wait_ge(gate_aT, g + 1)
                link(v.tensor_copy(aT[:].rearrange("p b h -> p (b h)"), bank[2][:, 0:GB * H1]))
                for s in range(H1 + 1):
                    if s < H1:
                        dve.wait_ge(mx_bc, g * H1 + s + 1)
                        if s >= 2:
                            dve.wait_ge(c_done, g * H1 + s - 1)
                        for b in range(GB):
                            last = v.scalar_tensor_tensor(rows(wk[s % 2])[:, b], rows(bank[4 + s % 2])[:, b],
                                                          aT[:, b, s:s + 1], mask_ji[:], ALU.add, ALU.add)
                        last.then_inc(arg_done, 1)
                    h = s - 1
                    if h >= 0:
                        dve.wait_ge(dmat, g * H1 + h + 1)
                        dve.wait_ge(qk1, g * H1 + h + 1)
                        if h >= 2:
                            dve.wait_ge(num, g * H1 + h - 1)
                        v.tensor_tensor(wk[4 + h % 2][:], bank[6 + h % 2][:], wk[h % 2][:],
                                        ALU.mult).then_inc(c_done, 1)
                dve.wait_ge(num, g * H1 + H1)
                dve.wait_ge(gate_eM, g + 1)
                nv = [bank[2 + i][:, 0:2 * H1 * (DH1 + 1)].rearrange("p (b h d) -> p b h d", b=2, h=H1)
                      for i in range(2)]
                for i in range(2):
                    last = v.tensor_copy(den[:, 2 * i:2 * i + 2], nv[i][:, :, :, DH1])
                link(last)
                link(v.scalar_tensor_tensor(rden[:], den[:], -1.0, den[:], ALU.mult, ALU.max))
                link(v.tensor_tensor(den[:], rden[:], eM[:], ALU.max))
                link(v.tensor_scalar(den[:], den[:], 1.0e-6, None, ALU.add))
                link(v.reciprocal(rden[:], den[:]))
                hr = act_row[1][:].rearrange("p b (h d) -> p b h d", h=H1)
                for i in range(2):
                    last = v.tensor_tensor(hr[:, 2 * i:2 * i + 2], nv[i][:, :, :, 0:DH1],
                                           rden[:, 2 * i:2 * i + 2].unsqueeze(3).broadcast_to([128, 2, H1, DH1]),
                                           ALU.mult)
                link(last)
                norm(g, 1, act_row[1], resid, done=ln_out)
                dve.wait_ge(ln_out, g * LNS + 3)
                link(v.tensor_tensor(resid, resid, res["ln_scale"][:].unsqueeze(1).broadcast_to([128, GB, D]),
                                     ALU.mult))
                link(v.tensor_tensor(resid, resid, act_row[0][:], ALU.add))
                norm(g, 2, resid, act_row[1], done=ln_out)

                link(v.tensor_reduce(csum[:], rows(ctx_T), X, ALU.add))
                v.tensor_scalar(cbc[:], csum[:].unsqueeze(2).broadcast_to([128, GB, N]), 1.0 / N, None,
                                ALU.mult).then_inc(ctx_mean, 1)
                pr, oh1, oh2, t, ex, _ = (r[:] for r in rt)
                m1, m2, r, ssum, rs, _ = (q[:] for q in r1)
                dve.wait_ge(rt_logit, g + 1)
                link(v.tensor_tensor(pr, bank[7][:, 0:32].rearrange("p (b e) -> p b e", b=GB),
                                     res["gate_b0"][:].unsqueeze(1).broadcast_to([128, GB, E0]), ALU.add))
                link(v.tensor_reduce(m1, pr, X, ALU.max))
                v.tensor_tensor(t, pr, bc(m1), ALU.subtract).then_inc(rt_v, 1)
                dve.wait_ge(rt_a, g + 1)
                link(v.tensor_reduce(ssum, ex, X, ALU.add))
                link(v.reciprocal(rs, ssum))
                link(v.tensor_tensor(pr, ex, bc(rs), ALU.mult))
                top2(pr, oh1, oh2, m1, m2, t, r)
                link(v.tensor_tensor(ssum, m1, m2, ALU.add))
                link(v.tensor_scalar(ssum, ssum, 1.0e-9, None, ALU.add))
                link(v.reciprocal(rs, ssum))
                link(v.tensor_tensor(oh1, oh1, bc(m1), ALU.mult))
                link(v.tensor_tensor(oh2, oh2, bc(m2), ALU.mult))
                link(v.tensor_tensor(oh1, oh1, oh2, ALU.add))
                v.tensor_tensor(wexp[:], oh1, bc(rs), ALU.mult).then_inc(rt_w, 1)
                dve.wait_ge(rt_w, g + 1)
                acc = resid
                for e in range(E0S):
                    if e == 1:
                        dve.wait_ge(rt_wT, g + 1)
                        v.tensor_copy(wexpT[:], bank[6][0:8, :]).then_inc(rt_wT_sb, 1)
                    if e == 2:
                        dve.wait_ge(rt_bias, g + 1)
                        link(v.tensor_tensor(acc[:], rows(bank[7]), acc[:], ALU.add))
                    dve.wait_ge(down, g * E0S + e + 1)
                    y = rows(bank[4 + e % 2])
                    if e == 0:
                        dve.wait_ge(xb_done, g * 2 + 2)
                        v.tensor_tensor(acc[:], y, rows(wk[10]), ALU.add).then_inc(moe_acc, 1)
                    else:
                        for b in range(GB):
                            last = v.scalar_tensor_tensor(acc[:, b], y[:, b], wexp[:, b, e - 1:e], acc[:, b],
                                                          ALU.mult, ALU.add)
                        last.then_inc(moe_acc, 1)
                    dve.wait_ge(moe_acc, g * E0S + e + 1)
                norm(g, 3, resid, act_row[0], done=ln_out)

                dve.wait_ge(qkv2, g * 3 + 2)
                v.tensor_scalar(wk[0][:], bank[0][:], q_scale[:], None, ALU.mult).then_inc(q2_sb, 1)
                for s in range(H2):
                    dve.wait_ge(s2, g * H2 + s + 1)
                    S = rows(bank[4 + s % 2])
                    link(v.tensor_reduce(negmax[:, s % 2, :], S, X, ALU.max, negate=True))
                    if s >= 3:
                        dve.wait_ge(pT2, g * H2 + s - 2)
                    v.tensor_tensor(rows(wk[4 + s % 3]), S, negmax[:, s % 2, :].unsqueeze(2)
                                    .broadcast_to([128, GB, N]), ALU.add).then_inc(z2, 1)
                dve.wait_ge(o2, g * H2 + H2)
                ov = [bank[6 + i][:, 0:2 * H2 * (DH2 + 1)].rearrange("p (b h d) -> p b h d", b=2, h=H2)
                      for i in range(2)]
                for i in range(2):
                    last = v.reciprocal(den2[:, 2 * i:2 * i + 2], ov[i][:, :, :, DH2])
                link(last)
                orow = rows(wk[9]).rearrange("p b (h d) -> p b h d", h=H2)
                for i in range(2):
                    last = v.tensor_tensor(orow[:, 2 * i:2 * i + 2], ov[i][:, :, :, 0:DH2],
                                           den2[:, 2 * i:2 * i + 2].unsqueeze(3).broadcast_to([128, 2, H2, DH2]),
                                           ALU.mult)
                last.then_inc(o2_row, 1)
                dve.wait_ge(y2, g + 1)
                link(v.tensor_tensor(resid, rows(bank[3]), act_row[0][:], ALU.add))
                link(v.tensor_tensor(resid, resid, res["bout"][:].unsqueeze(1).broadcast_to([128, GB, D]),
                                     ALU.add))
                norm(g, 4, resid, act_row[1], done=ln_out)
                dve.wait_ge(y3, g + 1)
                link(v.tensor_tensor(resid, rows(bank[1]), act_row[1][:], ALU.add))
                link(v.tensor_tensor(resid, resid, res["xb"][:].unsqueeze(1).broadcast_to([128, GB, D]),
                                     ALU.add))
                norm(g, 5, resid, act_row[0], done=ln_out)

                dve.wait_ge(rl_logit, g + 1)
                v.tensor_tensor(logit1[:, bass.ds(g, 1)].rearrange("p g b e -> p (g b) e"),
                                bank[3][:, 0:GB * E1].rearrange("p (b e) -> p b e", b=GB),
                                res["lb_bias"][:].unsqueeze(1).broadcast_to([128, GB, E1]),
                                ALU.add).then_inc(rl_v, 1)

            restart()
            dve.wait_ge(rl_a, 1)
            half_tiles = [work[:, i * B * E1:(i + 1) * B * E1].rearrange("p (b e) -> p b e", b=B) for i in range(5)]
            ex, pr, oh1, oh2, t = half_tiles
            m1, m2, r, ssum, rs = (wk[5][:, i * B:(i + 1) * B] for i in range(5))
            link(v.tensor_scalar(ex, ex, 1.0, None, ALU.add))
            link(v.reciprocal(pr, ex))
            top2(pr, oh1, oh2, m1, m2, t, r)
            link(v.tensor_tensor(ssum, m1, m2, ALU.add))
            link(v.tensor_scalar(ssum, ssum, 1.0e-8, None, ALU.add))
            link(v.reciprocal(rs, ssum))
            link(v.tensor_tensor(sel1[:].rearrange("p g b e -> p (g b) e"), oh1, oh2, ALU.add))
            link(v.tensor_tensor(oh1, oh1, bc(m1), ALU.mult))
            link(v.tensor_tensor(oh2, oh2, bc(m2), ALU.mult))
            link(v.tensor_tensor(oh1, oh1, oh2, ALU.add))
            link(v.tensor_tensor(oh1, oh1, bc(rs), ALU.mult))
            v.tensor_reduce(router_sum[:, 0], sel1[:].rearrange("p g b e -> p e (g b)"), X, ALU.add)
            v.tensor_reduce(router_sum[:, 1], oh1.rearrange("p b e -> p e b"), X, ALU.add).then_inc(sums_done, 1)

            restart()
            dve.wait_ge(tot, 1)
            link(v.tensor_copy(wmean[:, 0:2], bank[0][0:8, 0:2]))
            link(v.tensor_scalar(wmean[:, 0:1], wmean[:, 0:1], 1.0, None, ALU.max))
            link(v.reciprocal(wmean[:, 2:3], wmean[:, 0:1]))
            v.tensor_tensor(wmean[:, 3:4], wmean[:, 1:2], wmean[:, 2:3], ALU.mult).then_inc(f_out, 1)
            dve.wait_ge(f_out, 1)
            with dve.Fori(0, G) as g:
                restart()
                dve.wait_ge(selT_ps, g + 1)
                v.tensor_scalar(selT[:], bank[5][0:8, :], wmean[:, 3:4], None, ALU.mult).then_inc(selT_sb, 1)
                for p in range(BLK):
                    dve.wait_ge(silu, g * BLK + p + 1)
                    hid = wk[2 + p]
                    if p < PAIRS:
                        link(v.tensor_tensor(hid[:], bank[2 + p % 2][:], wk[p % 2][:], ALU.mult))
                        v.tensor_tensor(hid[:], bank[4 + p % 2][:], hid[:], ALU.mult).then_inc(h_done, 1)
                    else:
                        v.tensor_tensor(hid[:], bank[2 + p % 2][:], wk[p % 2][:], ALU.mult).then_inc(h_done, 1)
                dve.wait_ge(y4, g + 1)
                link(v.tensor_tensor(resid, rows(bank[7]), x_row[:], ALU.add))
                norm(g, 0, resid, act_row[0], f_stats, f_rstd, 1, f_out)

        @block.scalar
        def _(act):
            count = [0]

            def link(ins):
                count[0] += 1
                ins.then_inc(chain_a, 1)
                act.wait_ge(chain_a, count[0])

            def restart():
                act.sem_clear(chain_a)
                count[0] = 0

            def fn(o, i, f, **k):
                return nc.scalar.activation(o, i, f, **k)

            restart()
            act.preload_act_table_set("natural_log_exp_and_others")
            act.wait_ge(par_v, 1)
            link(fn(p_abs[:], p_abs[:], ACT.Exp))
            fn(p_abs[:], p_abs[:], ACT.Ln, bias=1.0).then_inc(par_a, 1)
            fn(p_sig[:], par[:, 80:97], ACT.Exp, scale=-1.0).then_inc(par_a, 1)
            act.wait_ge(par_v, 2)
            fn(sinT[:], wgt[:], ACT.Sin).then_inc(par_a, 1)
            act.wait_ge(par_v, 3)
            fn(cosT[:], dec_inv[:], ACT.Sin).then_inc(par_a, 1)
            act.preload_act_table_set("natural_log_exp_and_others")
            act.wait_ge(par_a, 4)
            act.wait_ge(par_v, 4)
            link(fn(dec_inv[:], dec[:], ACT.Exp, scale=-1.0))
            fn(dec[:], dec[:], ACT.Exp).then_inc(par_a, 1)
            act.wait_ge(par_v, 5)
            link(fn(bias_t[:], bias_t[:], ACT.Ln))
            fn(wgt[:], bias_t[:], ACT.Exp, scale=-1.0).then_inc(par_a, 1)
            for c in range(4):
                act.wait_ge(fold, c + 1)
                fn(vo[:, 4 * c:4 * c + 4].rearrange("p h d -> p (h d)"), bank[c][:], ACT.Copy).then_inc(fold_sb, 1)

            def norm(g, i, stats=ln_stats, rs=ln_rstd, per=LNS):
                act.wait_ge(stats, g * per + i + 1)
                link(fn(ln_t[:], mv[:, :, 1], ACT.Ln, bias=res["cols"][:, 5:6]))
                fn(rstd[:], ln_t[:], ACT.Exp, scale=-0.5).then_inc(rs, 1)

            def to_T(g, i, src_bank):
                act.wait_ge(act_tr, g * 5 + i + 1)
                fn(act_T[:], src_bank[:], ACT.Copy).then_inc(act_T_sb, 1)

            with act.Fori(0, G) as g:
                restart()
                for s in range(H0 + 7):
                    h = s - 4
                    if 0 <= h < H0:
                        act.wait_ge(logits, g * H0 + h + 1)
                        if h >= 3:
                            act.wait_ge(prob_T, g * H0 + h - 2)
                        P = rows(wk[13 + h % 3])
                        for b in range(GB):
                            last = fn(P[:, b], rows(wk[12])[:, b], ACT.Exp, bias=negmax[:, h % 2, b:b + 1],
                                      accum_out=esum[:, h % 4, b:b + 1])
                        last.then_inc(exped, 1)
                    h = s - 1
                    if 0 <= h < H0:
                        act.wait_ge(qk_rot, g * 2 * H0 + 2 * h + 2)
                        fn(wk[8][:], wk[4 + h % 2][:], ACT.Square)
                        fn(wk[9][:], wk[6 + h % 2][:], ACT.Square).then_inc(squares, 1)
                    h = s - 5
                    if 0 <= h < H0:
                        act.wait_ge(v_proj, g * H0 + h + 1)
                        if h >= 3:
                            act.wait_ge(head_out, g * H0 + h - 2)
                        fn(wk[16 + h % 3][:], bank[2][:], ACT.Copy).then_inc(v_sb, 1)
                    h = s - 6
                    if 0 <= h < H0:
                        act.wait_ge(prob_T, g * H0 + h + 1)
                        if h >= 2:
                            act.wait_ge(head_out, g * H0 + h - 1)
                        fn(wk[19 + h % 2][:], bank[6][:], ACT.Copy).then_inc(prob_T_sb, 1)
                    h = s - 1
                    if 0 <= h < H0:
                        act.wait_ge(norms, g * H0 + h + 1)
                        fn(nrm[:, h % 2, :], bank[3][:, 0:8], ACT.Copy).then_inc(norms_sb, 1)
                    h = s - 2
                    if 0 <= h < H0:
                        act.wait_ge(maha, g * H0 + h + 1)
                        fn(wk[(11, 21)[h % 2]][:], wk[(11, 21)[h % 2]][:], ACT.Ln, bias=1.0).then_inc(log_done, 1)
                norm(g, 0)
                to_T(g, 0, bank[4])
                act.wait_ge(gate_v, g + 1)
                link(fn(gate[1][:], gate[0][:], ACT.Exp))
                fn(gate[1][:], gate[1][:], ACT.Ln, bias=res["cols"][0:8, 6:7]).then_inc(gate_a, 1)
                for h in range(H1):
                    act.wait_ge(arg_done, g * H1 + h + 1)
                    fn(wk[h % 2][:], wk[h % 2][:], ACT.Exp).then_inc(dmat, 1)
                act.wait_ge(gate_T, g + 1)
                fn(eM[:].rearrange("p b h -> p (b h)"), bank[0][:, 0:GB * H1], ACT.Exp, scale=-1.0).then_inc(gate_eM, 1)
                norm(g, 1)
                norm(g, 2)
                to_T(g, 1, bank[6])
                act.wait_ge(rt_v, g + 1)
                fn(rt[4][:], rt[3][:], ACT.Exp).then_inc(rt_a, 1)
                for e in range(E0S):
                    for c in range(CH):
                        act.wait_ge(up, g * E0S * CH + e * CH + c + 1)
                        if e >= 2:
                            act.wait_ge(down, g * E0S + e - 1)
                        fn(wk[4 * (e % 2) + c][:], bank[c][:], ACT.Gelu_apprx_tanh,
                           bias=res["b_up"][:, e, c:c + 1]).then_inc(gelu, 1)
                act.preload_act_table_set("natural_log_exp_and_others")
                norm(g, 3)
                to_T(g, 2, bank[6])
                act.wait_ge(qkv2, g * 3 + 1)
                fn(wk[1][:], bank[1][:], ACT.Copy).then_inc(kv2_sb, 1)
                act.wait_ge(qkv2, g * 3 + 3)
                fn(v2[:, :, :, 0:DH2], bank[2][:].rearrange("p (b h d) -> p b h d", b=GB, h=H2),
                   ACT.Copy).then_inc(kv2_sb, 1)
                for s in range(H2 + 2):
                    if s < H2:
                        act.wait_ge(z2, g * H2 + s + 1)
                        fn(wk[4 + s % 3][:], wk[4 + s % 3][:], ACT.Exp).then_inc(p2, 1)
                    h = s - 2
                    if h >= 0:
                        act.wait_ge(pT2, g * H2 + h + 1)
                        if h >= 2:
                            act.wait_ge(o2, g * H2 + h - 1)
                        fn(wk[7 + h % 2][:], bank[2 + h % 2][:], ACT.Copy).then_inc(pT2_sb, 1)
                act.wait_ge(o2_tr, g + 1)
                fn(wk[10][:], bank[2][:], ACT.Copy).then_inc(o2_T, 1)
                norm(g, 4)
                to_T(g, 3, bank[0])
                norm(g, 5)
                to_T(g, 4, bank[2])

            act.wait_ge(rl_v, G)
            fn(work[:, 0:B * E1], logit1[:].rearrange("p g b e -> p (g b e)"), ACT.Exp, scale=-1.0).then_inc(rl_a, 1)

            act.wait_ge(sums_done, 1)
            with act.Fori(0, G) as g:
                restart()
                fn(sel[:], sel1[:, bass.ds(g, 1)].rearrange("p g b e -> p (g b) e"), ACT.Copy).then_inc(sel_here, 1)
                for p in range(BLK):
                    act.wait_ge(gup, g * BLK + p + 1)
                    if p >= 2:
                        act.wait_ge(h_done, g * BLK + p - 1)
                    fn(wk[p % 2][:], bank[p % 2][:], ACT.Silu).then_inc(silu, 1)
                act.preload_act_table_set("natural_log_exp_and_others")
                norm(g, 0, f_stats, f_rstd, 1)

        @block.gpsimd
        def _(pool):
            q = nc.gpsimd
            pool.wait_ge(loaded_first, 16 * len(for_tables))
            pool.wait_ge(loaded, 16 * len(rest))
            with pool.Fori(0, G) as g:
                for name, tile in (("x_T", x_T[:]), ("x_row", x_row[:].rearrange("p b d -> p (b d)"))):
                    q.dma_start(tile, a[name][bass.ds(g, 1)].rearrange("g p n -> (g p) n")).then_inc(in_x, 16)
                for s in range(H0 + 5):
                    if s < H0:
                        pool.wait_ge(q_parts, g * H0 + s + 1)
                        if s >= 2:
                            pool.wait_ge(score, g * H0 + s - 1)
                        q.tensor_tensor(wk[4 + s % 2][:], wk[0][:], wk[1][:], ALU.add).then_inc(qk_rot, 1)
                    h = s - 1
                    if 0 <= h < H0:
                        pool.wait_ge(norms_sb, g * H0 + h + 1)
                        if h >= 2:
                            pool.wait_ge(score, g * H0 + h - 1)
                        q.tensor_tensor(rows(wk[(22, 10)[h % 2]]), ident[:].unsqueeze(1).broadcast_to([128, GB, N]),
                                        nrm[:, h % 2, 0:4].unsqueeze(2).broadcast_to([128, GB, N]),
                                        ALU.mult).then_inc(diag_done, 1)
                    if s < H0:
                        pool.wait_ge(k_parts, g * H0 + s + 1)
                        q.tensor_tensor(wk[6 + s % 2][:], wk[2][:], wk[3][:], ALU.add).then_inc(qk_rot, 1)
                    h = s - 5
                    if 0 <= h < H0:
                        pool.wait_ge(sums_inv, g * H0 + h + 1)
                        P = rows(wk[13 + h % 3])
                        q.tensor_tensor(P, P, rsum[:, h % 2, :].unsqueeze(2).broadcast_to([128, GB, N]),
                                        ALU.mult).then_inc(prob, 1)
                pool.wait_ge(in_ctx, g * 32 + 32)
                for h in range(H1):
                    if h >= 2:
                        pool.wait_ge(qk1, g * H1 + h - 1)
                    q.tensor_tensor(wk[2 + h % 2][:], ctx_T[:], head_mask1[:, h:h + 1].broadcast_to([128, W]),
                                    ALU.mult).then_inc(ctx_masked, 1)
                pool.wait_ge(ln_out, g * LNS + 4)
                q.tensor_tensor(rows(wk[10]), act_row[1][:],
                                res["b_sh"][:].unsqueeze(1).broadcast_to([128, GB, D]), ALU.add).then_inc(xb_done, 1)
                pool.wait_ge(xb_done, g * 2 + 1)
                q.tensor_tensor(rows(wk[10]), rows(wk[10]), act_row[1][:], ALU.add).then_inc(xb_done, 1)
                for h in range(H2):
                    pool.wait_ge(kv2_sb, g * 2 + 1)
                    if h >= 2:
                        pool.wait_ge(s2, g * H2 + h - 1)
                    q.tensor_tensor(wk[2 + h % 2][:], wk[1][:], head_mask2[:, h:h + 1].broadcast_to([128, W]),
                                    ALU.mult).then_inc(k2_masked, 1)

        @block.tensor
        def _(pe):
            def mm(o, l, r, start=True, stop=True):
                return nc.tensor.matmul(o, l, r, start=start, stop=stop, skip_group_check=True)

            def transposes(dst, src, sem_out):
                for b in range(GB):
                    last = nc.tensor.transpose(rows(dst)[:, b], src[:, b], ident[:])
                last.then_inc(sem_out, 1)

            pe.wait_ge(loaded_first, 16 * len(for_tables))
            pe.wait_ge(loaded, 16 * len(rest))
            for c in range(4):
                for h in range(4 * c, 4 * c + 4):
                    last = mm(rows(bank[c])[:, h % 4], res["wvT0"][:, h], res["wo0"][:, h], start=h % 4 == 0)
                last.then_inc(fold, 1)
            pe.wait_ge(fold_sb, 4)
            pe.wait_ge(tables, 1)
            with pe.Fori(0, G) as g:
                pe.wait_ge(in_x, g * 32 + 32)
                for s in range(H0 + 7):
                    if s < H0:
                        if s > 0:
                            pe.wait_ge(q_parts, g * H0 + s)
                        mm(bank[0][:], res["wq0"][:, s], x_T[:]).then_inc(q_proj, 1)
                        if s > 0:
                            pe.wait_ge(k_parts, g * H0 + s)
                        mm(bank[1][:], res["wk0"][:, s], x_T[:]).then_inc(k_proj, 1)
                    h = s - 2
                    if 0 <= h < H0:
                        pe.wait_ge(diag_done, g * H0 + h + 1)
                        if h >= 2:
                            pe.wait_ge(maha, g * H0 + h - 1)
                        S = bank[4 + h % 2]
                        mm(S[:], dec[:, h], wk[(22, 10)[h % 2]][:], stop=False)
                        for b in range(GB):
                            last = mm(rows(S)[:, b], rows(wk[4 + h % 2])[:, b], rows(wk[6 + h % 2])[:, b],
                                      start=False)
                        last.then_inc(score, 1)
                    h = s - 5
                    if 0 <= h < H0:
                        if h > 0:
                            pe.wait_ge(v_sb, g * H0 + h)
                        for b in range(GB):
                            last = mm(rows(bank[2])[:, b], rows(x_T)[:, b], vo[:, h], start=b == 0)
                        last.then_inc(v_proj, 1)
                    h = s - 7
                    if h >= 0:
                        pe.wait_ge(prob_T_sb, g * H0 + h + 1)
                        pe.wait_ge(v_sb, g * H0 + h + 1)
                        for b in range(GB):
                            last = mm(rows(bank[7])[:, b], rows(wk[19 + h % 2])[:, b], rows(wk[16 + h % 3])[:, b],
                                      start=h == 0 and b == 0, stop=h == H0 - 1)
                        last.then_inc(head_out, 1)
                    h = s - 6
                    if 0 <= h < H0:
                        pe.wait_ge(prob, g * H0 + h + 1)
                        if h > 0:
                            pe.wait_ge(prob_T_sb, g * H0 + h)
                        transposes(bank[6], rows(wk[13 + h % 3]), prob_T)
                    h = s - 1
                    if 0 <= h < H0:
                        pe.wait_ge(squares, g * H0 + h + 1)
                        if h > 0:
                            pe.wait_ge(norms_sb, g * H0 + h)
                        for b in range(GB):
                            mm(bank[3][:, b:b + 1], rows(wk[9])[:, b], half_col, start=b == 0)
                            last = mm(bank[3][:, 4 + b:5 + b], rows(wk[8])[:, b], half_col, start=False)
                        last.then_inc(norms, 1)
                pe.wait_ge(in_ctx, g * 32 + 32)
                gw = res["gate_w"]
                mm(bank[0][0:40, :], gw[:, 1], ctx_T[:], stop=False)
                pe.wait_ge(ln_out, g * LNS + 2)
                transposes(bank[4], act_row[0], act_tr)
                pe.wait_ge(act_T_sb, g * 5 + 1)
                mm(bank[0][0:40, :], gw[:, 0], act_T[:], start=False).then_inc(gates, 1)

                def gate_columns(dst, src, sem_out):
                    for b in range(GB):
                        last = mm(dst[:, b * H1:b * H1 + H1], src[:, b * N:b * N + N], ident[0:8, 0:8], start=b == 0)
                    last.then_inc(sem_out, 1)
                pe.wait_ge(gate_rows, g + 1)
                gate_columns(bank[2], gate[4], gate_aT)
                nv = [bank[2 + i][:, 0:2 * H1 * (DH1 + 1)].rearrange("p (b h d) -> p b h d", b=2, h=H1)
                      for i in range(2)]
                for s in range(H1 + 2):
                    if s < H1:
                        if s >= 2:
                            pe.wait_ge(arg_done, g * H1 + s - 1)
                        else:
                            pe.wait_ge(gate_max, g + 1)
                        mm(bank[4 + s % 2][:], sel24[:, s], m_parts[:]).then_inc(mx_bc, 1)
                        pe.wait_ge(ctx_masked, g * H1 + s + 1)
                        if s >= 2:
                            pe.wait_ge(c_done, g * H1 + s - 1)
                        for b in range(GB):
                            last = mm(rows(bank[6 + s % 2])[:, b], rows(wk[2 + s % 2])[:, b], rows(act_T)[:, b],
                                      start=b == 0)
                        last.then_inc(qk1, 1)
                    if s == H1:
                        pe.wait_ge(gate_tot, g + 1)
                        gate_columns(bank[0], gate[3], gate_T)
                    h = s - 2
                    if h >= 0:
                        pe.wait_ge(c_done, g * H1 + h + 1)
                        for b in range(GB):
                            last = mm(nv[b // 2][:, b % 2, h, :], rows(wk[4 + h % 2])[:, b], v1[:, b, h, :],
                                      start=h == 0 and b % 2 == 0)
                        last.then_inc(num, 1)
                pe.wait_ge(ln_out, g * LNS + 4)
                transposes(bank[6], act_row[1], act_tr)
                pe.wait_ge(act_T_sb, g * 5 + 2)
                for b in range(GB):
                    last = mm(bank[7][:, b * E0:b * E0 + E0], rows(act_T)[:, b], res["gw0"][:], start=b == 0)
                last.then_inc(rt_logit, 1)
                for s in range(E0S + 1):
                    if s < E0S:
                        for c in range(CH):
                            if s > 0:
                                pe.wait_ge(gelu, g * E0S * CH + (s - 1) * CH + c + 1)
                            mm(bank[c][:], res["w_up"][:, s, c * 128:c * 128 + 128], act_T[:]).then_inc(up, 1)
                    e = s - 1
                    if e >= 0:
                        pe.wait_ge(gelu, g * E0S * CH + e * CH + CH)
                        if e >= 2:
                            pe.wait_ge(moe_acc, g * E0S + e - 1)
                        for b in range(GB):
                            for c in range(CH):
                                last = mm(rows(bank[4 + e % 2])[:, b], rows(wk[4 * (e % 2) + c])[:, b],
                                          res["w_down"][:, e, c], start=b == 0 and c == 0)
                        last.then_inc(down, 1)
                    if e == 0:
                        pe.wait_ge(rt_w, g + 1)
                        for b in range(GB):
                            last = nc.tensor.transpose(bank[6][0:8, b * N:b * N + N], wexp[:, b], ident[:])
                        last.then_inc(rt_wT, 1)
                    if e == 1:
                        pe.wait_ge(rt_wT_sb, g + 1)
                        for b in range(GB):
                            last = mm(rows(bank[7])[:, b], wexpT[:, b * N:b * N + N], res["b_down"][:],
                                      start=b == 0)
                        last.then_inc(rt_bias, 1)
                pe.wait_ge(ln_out, g * LNS + 5)
                transposes(bank[6], act_row[0], act_tr)
                pe.wait_ge(act_T_sb, g * 5 + 3)
                mm(bank[1][:], res["wk2"][:], act_T[:]).then_inc(qkv2, 1)
                mm(bank[0][:], res["wq2"][:], act_T[:]).then_inc(qkv2, 1)
                for b in range(GB):
                    last = mm(rows(bank[2])[:, b], rows(act_T)[:, b], res["wv2"][:], start=b == 0)
                last.then_inc(qkv2, 1)
                pe.wait_ge(q2_sb, g + 1)
                ov = [bank[6 + i][:, 0:2 * H2 * (DH2 + 1)].rearrange("p (b h d) -> p b h d", b=2, h=H2)
                      for i in range(2)]
                for s in range(H2 + 3):
                    if s < H2:
                        pe.wait_ge(k2_masked, g * H2 + s + 1)
                        if s >= 2:
                            pe.wait_ge(z2, g * H2 + s - 1)
                        for b in range(GB):
                            last = mm(rows(bank[4 + s % 2])[:, b], rows(wk[0])[:, b], rows(wk[2 + s % 2])[:, b],
                                      start=b == 0)
                        last.then_inc(s2, 1)
                    h = s - 2
                    if 0 <= h < H2:
                        pe.wait_ge(p2, g * H2 + h + 1)
                        if h >= 2:
                            pe.wait_ge(pT2_sb, g * H2 + h - 1)
                        else:
                            pe.wait_ge(kv2_sb, g * 2 + 2)
                        transposes(bank[2 + h % 2], rows(wk[4 + h % 3]), pT2)
                    h = s - 3
                    if h >= 0:
                        pe.wait_ge(pT2_sb, g * H2 + h + 1)
                        for b in range(GB):
                            last = mm(ov[b // 2][:, b % 2, h, :], rows(wk[7 + h % 2])[:, b], v2[:, b, h, :],
                                      start=h == 0 and b % 2 == 0)
                        last.then_inc(o2, 1)
                pe.wait_ge(o2_row, g + 1)
                transposes(bank[2], rows(wk[9]), o2_tr)
                pe.wait_ge(o2_T, g + 1)
                for b in range(GB):
                    last = mm(rows(bank[3])[:, b], rows(wk[10])[:, b], res["wout2"][:], start=b == 0)
                last.then_inc(y2, 1)
                pe.wait_ge(ctx_mean, g + 1)
                for b in range(GB):
                    mm(rows(bank[1])[:, b], cbc[:, b], res["w2x"][:], start=b == 0, stop=False)
                pe.wait_ge(ln_out, g * LNS + 6)
                transposes(bank[0], act_row[1], act_tr)
                pe.wait_ge(act_T_sb, g * 5 + 4)
                for b in range(GB):
                    last = mm(rows(bank[1])[:, b], rows(act_T)[:, b], res["w1x"][:], start=False)
                last.then_inc(y3, 1)
                pe.wait_ge(ln_out, g * LNS + 7)
                transposes(bank[2], act_row[0], act_tr)
                pe.wait_ge(act_T_sb, g * 5 + 5)
                for b in range(GB):
                    last = mm(bank[3][:, b * E1:b * E1 + E1], rows(act_T)[:, b], res["gw1"][:], start=b == 0)
                last.then_inc(rl_logit, 1)

            pe.wait_ge(sums_done, 1)
            mm(bank[0][0:8, 0:1], router_sum[:, 0], ones_col)
            mm(bank[0][0:8, 1:2], router_sum[:, 1], ones_col, start=False).then_inc(tot, 1)
            with pe.Fori(0, G) as g:
                pe.wait_ge(sel_here, g + 1)
                for b in range(GB):
                    last = nc.tensor.transpose(bank[5][0:8, b * N:b * N + N], sel[:, b], ident[:])
                last.then_inc(selT_ps, 1)
                pe.wait_ge(in2, g * 32 + 32 + 16 * len(phase2))
                for s in range(BLK + 1):
                    p = s
                    if p < BLK:
                        if p >= 2:
                            pe.wait_ge(h_done, g * BLK + p - 1)
                        elif p == 0:
                            pe.wait_ge(f_out, g + 1)
                        mm(bank[2 + p % 2][:], late["w_u1"][:, p], x_T[:])
                        last = mm(bank[p % 2][:], late["w_g1"][:, p], x_T[:])
                        if p < PAIRS:
                            pe.wait_ge(selT_sb, g + 1)
                            last = mm(bank[4 + p % 2][:], late["sel2"][:, p], selT[:])
                        last.then_inc(gup, 1)
                    p = s - 1
                    if p >= 0:
                        pe.wait_ge(h_done, g * BLK + p + 1)
                        for b in range(GB):
                            last = mm(rows(bank[7])[:, b], rows(wk[2 + p])[:, b], late["w_d1"][:, p],
                                      start=p == 0 and b == 0, stop=p == BLK - 1)
                last.then_inc(y4, 1)


def layouts(inp):
    import numpy as np
    f = {k: np.asarray(v) for k, v in inp.items()}
    c = np.ascontiguousarray

    def row_groups(x):
        return c(x.reshape(G, GB, N, D).transpose(0, 2, 1, 3).reshape(G, N, W))

    def T_groups(x):
        return c(x.reshape(G, GB, N, D).transpose(0, 3, 1, 2).reshape(G, D, W))

    def tile(v):
        return c(np.tile(v.reshape(1, -1), (128, 1)))

    def heads(w, parts):
        r = w.reshape(D, 2, H0, DH0)
        return c(np.stack([r[:, p] for p in parts], 2).reshape(D, H0, len(parts) * DH0))

    def spread(i_gate, f_gate, shape):
        r = np.zeros((40,) + shape[1:], i_gate.dtype)
        r[0:8], r[32:40] = i_gate.reshape(shape), f_gate.reshape(shape)
        return r

    i = np.arange(128)
    f32 = np.float32
    cols = np.zeros((128, 40), f32)
    cols[:, 0] = np.where((i < 64) == (i % 64 < 32), -1, 1)
    cols[:, 1], cols[:, 2] = i < H2T * DH2, i >= H2T * DH2
    cols[:, 3], cols[:, 4], cols[:, 5], cols[:, 6] = 1, -0.5, 1e-5, 1
    cols[:, 8:16] = (i[:, None] // DH1 == np.arange(H1)) * DH1 ** -0.5
    cols[:, 16:32] = i[:, None] // DH2 == np.arange(H2)
    cols[:, 32:40] = 8 - np.arange(8)
    e = np.arange(8)
    a = dict(
        x_row=row_groups(f["x"]), x_T=T_groups(f["x"]),
        ctx_row=row_groups(f["ctx_1024"]), ctx_T=T_groups(f["ctx_1024"]),
        ident=np.eye(128, dtype=f32),
        dist=np.abs(i[:, None] - i).astype(f32),
        mask_ij=np.where(i[:, None] >= i, 0, NEG).astype(f32),
        mask_ji=np.where(i[:, None] <= i, 0, NEG).astype(f32),
        tramp=c(np.tile(i.astype(f32), (128, 1))),
        cols=cols,
        par=tile(np.concatenate([f["L0_attn_" + k] for k in
                                 ("sigma_raw", "eta_raw", "gamma_raw", "nu_raw", "tau", "mu_raw")]
                                + [f["L1_attn_w_sigma"]])),
        freq=c(np.tile(f["L0_attn_omega"].T, (4, 1))),
        wq0=heads(f["L0_attn_Wq"], (0, 1)), wk0=heads(f["L0_attn_Wk"], (0, 1)),
        wvT0=c(f["L0_attn_Wv"].T.reshape(2, H0, DH0, D).transpose(0, 2, 1, 3).reshape(128, H0, D)),
        wo0=c(f["L0_attn_Wo"].reshape(2, H0, DH0, D).transpose(0, 2, 1, 3).reshape(128, H0, D)),
        gate_w=spread(f["L0_xattn_igate_w"], f["L0_xattn_fgate_w"], (H1, 3, D)).transpose(2, 1, 0).copy(),
        gate_b=spread(f["L0_xattn_igate_b"], f["L0_xattn_fgate_b"], (H1, 1)),
        ln_scale=tile(f["L0_xattn_ln_scale"]),
        sel24=c(np.broadcast_to(-1.0 * (np.arange(72)[:, None] % 32 == e)[:, :, None], (72, 8, 128)).astype(f32)),
        gw0=c(f["L0_ffn_gate_w"]), gate_b0=tile(f["L0_ffn_gate_b"]),
        w_up=c(np.concatenate([f["L0_ffn_sh_w1"][None], f["L0_ffn_ew1"]]).transpose(1, 0, 2)),
        b_up=c(np.concatenate([f["L0_ffn_sh_b1"][None], f["L0_ffn_eb1"]]).reshape(E0S, CH, 128).transpose(2, 0, 1)),
        w_down=c(np.concatenate([f["L0_ffn_sh_w2"][None], f["L0_ffn_ew2"]])
                 .reshape(E0S, CH, 128, D).transpose(2, 0, 1, 3)),
        b_sh=tile(f["L0_ffn_sh_b2"]), b_down=c(f["L0_ffn_eb2"]),
        wq2=c(np.concatenate([f["L1_attn_Wqt"], f["L1_attn_Wqs"]], 1)),
        wk2=c(np.concatenate([f["L1_attn_Wkt"], f["L1_attn_Wks"]], 1)),
        wv2=c(f["L1_attn_Wv"]), wout2=c(f["L1_attn_Wout"]), bout=tile(f["L1_attn_bout"]),
        w1x=c(f["L1_xattn_W"][:, :D].T), w2x=c(f["L1_xattn_W"][:, D:].T), xb=tile(f["L1_xattn_b"]),
        gw1=c(f["L1_ffn_gate_w"].T), lb_bias=tile(f["L1_ffn_lb_bias"]),
        w_g1=c(np.concatenate([f["L1_ffn_expert_gate_w"].reshape(E1 * I1, D), f["L1_ffn_shared_gate_w"]])
               .reshape(BLK, 128, D).transpose(2, 0, 1)),
        w_u1=c(np.concatenate([f["L1_ffn_expert_up_w"].reshape(E1 * I1, D), f["L1_ffn_shared_up_w"]])
               .reshape(BLK, 128, D).transpose(2, 0, 1)),
        w_d1=c(np.concatenate([f["L1_ffn_expert_down_w"].transpose(0, 2, 1).reshape(E1 * I1, D),
                               f["L1_ffn_shared_down_w"].T]).reshape(BLK, 128, D).transpose(1, 0, 2)),
        sel2=c(np.broadcast_to((e[:, None, None] == (2 * np.arange(PAIRS)[:, None] + (i // 64))), (8, PAIRS, 128))
               .astype(f32)),
    )
    return a


def kernel(**inputs):
    import concourse.bacc as bacc
    from concourse.bass_utils import run_bass_kernel_spmd as run

    fp32 = mybir.dt.float32
    arrays = layouts(inputs)
    nc = bacc.Bacc("TRN2", target_bir_lowering=False, num_devices=1)
    aps = {k: nc.dram_tensor("in_" + k, v.shape, fp32, kind="ExternalInput").ap() for k, v in arrays.items()}
    out = nc.dram_tensor("out", (B, N, D), fp32, kind="ExternalOutput").ap()
    x5 = nc.dram_tensor("x5_scratch", (G, 128, W), fp32, kind="Internal").ap()
    x5T = nc.dram_tensor("x5T_scratch", (G, 128, W), fp32, kind="Internal").ap()
    decoder(nc, aps, out.rearrange("(g b) t d -> g b t d", b=GB), x5, x5T)
    r = run(nc, [{"in_" + k: v for k, v in arrays.items()}], core_ids=[0])
    return r.results[0]["out"]
```

```python
import math
from contextlib import ExitStack

import concourse.bass as bass
from concourse import mybir

B, N, D = 32, 128, 128
GB = 4
G = B // GB
W = GB * N
H0, DH0 = 16, 64
H1, DH1 = 8, 16
E0, I0 = 8, 512
CH = I0 // 128
E0S = E0 + 1
H2, DH2 = 16, 8
H2T = H2 // 4
E1, I1 = 8, 64
PAIRS = E1 * I1 // 128
BLK = PAIRS + 1
NEG = -1.0e30
LNS = 6


def decoder(nc, a, out, x5_scratch, x5T_scratch):
    fp32, bf16 = mybir.dt.float32, mybir.dt.bfloat16
    ALU = mybir.AluOpType
    ACT = mybir.ActivationFunctionType
    X = mybir.AxisListType.X

    with ExitStack() as ctx:
        def sb(name, *shape, dtype=fp32):
            return ctx.enter_context(nc.sbuf_tensor(name, list(shape), dtype))

        def sem(name):
            return ctx.enter_context(nc.semaphore(name))

        bank = [ctx.enter_context(nc.psum_tensor(f"bank{i}", [128, W], fp32)) for i in range(8)]

        def prob_T_bank(h):
            return 6 if h < H0 - 2 else h - (H0 - 2)

        def rows(ap, d=D):
            return ap[:, 0:GB * d].rearrange("p (b d) -> p b d", b=GB)

        work = sb("work", 128, 24 * W)
        wk = [work[:, i * W:(i + 1) * W] for i in range(24)]
        streamed = ("x_row", "x_T", "ctx_row", "ctx_T")
        phase2 = ("w_g1", "w_u1", "w_d1", "sel2")
        res = {name: sb("sb_" + name, *a[name].shape) for name in a
               if name not in streamed + phase2 + ("dist", "tramp", "wvT0", "wo0", "sel24")}
        res["dist"], res["tramp"] = wk[0][:, 0:N], wk[0][:, N:2 * N]
        res["sel24"] = work[0:72, 2 * W:4 * W].rearrange("p (h n) -> p h n", h=H1)
        sel24, m_parts = sb("sel24", 72, H1, 128, dtype=bf16), sb("m_parts", 72, W, dtype=bf16)
        res["wvT0"], res["wo0"] = (work[:, i * W:(i + 4) * W].rearrange("p (h d) -> p h d", h=H0) for i in (4, 8))
        for_tables = ("par", "cols", "tramp", "freq", "dist", "mask_ij")
        rest = [name for name in res if name not in for_tables]
        ident, dist, mask_ij, mask_ji, tramp, cols = (res[k] for k in
                                                      ("ident", "dist", "mask_ij", "mask_ji", "tramp", "cols"))
        sgn, top_rows, low_rows, ones_col, half_col = (cols[:, i:i + 1] for i in range(5))
        head_mask1 = cols[:, 8:16]
        head_mask2 = cols[:, 16:32]
        rank = cols[:, 32:40]

        table_space = sb("table_space", 128, 6 * H0 * N)
        cosT, sinT, dec, dec_inv, wgt, bias_t = (
            table_space[:, i * H0 * N:(i + 1) * H0 * N].rearrange("p (h n) -> p h n", h=H0) for i in range(6))
        x5T_all, x5_all = (table_space[:, i * G * W:(i + 1) * G * W].rearrange("p (g n) -> p g n", g=G)
                           for i in range(2))
        late, at = {}, 2 * G * W
        for name in phase2:
            shape = a[name].shape
            size = shape[1] * shape[2]
            late[name] = table_space[0:shape[0], at:at + size].rearrange("p (k n) -> p k n", k=shape[1])
            at += size
        vo = sb("vo", 128, H0, D)
        par = res["par"]
        p_abs = sb("p_abs", 128, 4 * H0)
        p_sp = sb("p_sp", 128, 4 * H0)
        p_sig = sb("p_sig", 128, H0 + 1)
        p_col = sb("p_col", 128, 7, H0)
        q_scale = sb("q_scale", 128, 1)

        ang, turns, red = (work[:, i * W:(i + 4) * W].rearrange("p (h n) -> p h n", h=H0) for i in (12, 16, 20))

        x_row, x_T, ctx_T = sb("x_row", 128, GB, D), sb("x_T", 128, W), sb("ctx_T", 128, W)
        v1 = sb("v1", 128, GB, H1, DH1 + 1)
        act_row = [sb(f"act_row{i}", 128, GB, D) for i in range(2)]
        act_T = sb("act_T", 128, W)
        resid = rows(wk[21])
        st, mv = sb("st", 128, GB, 6), sb("mv", 128, GB, 2)
        ln_t, rstd = sb("ln_t", 128, GB), sb("rstd", 128, GB)

        nrm = sb("nrm", 128, 2, 8)
        negmax = sb("negmax", 128, 2, GB)
        esum = sb("esum", 128, 4, GB)
        rsum = sb("rsum", 128, 2, GB)

        gate = [wk[6 + i][0:8, :] for i in range(6)] + [sb("gate_ones", 8, W)]
        aT, eM = sb("aT", 128, GB, H1), sb("eM", 128, GB, H1)
        den, rden = sb("den", 128, GB, H1), sb("rden", 128, GB, H1)
        rt = [sb(f"rt{i}", 128, GB, E0) for i in range(5)]
        r1 = [sb(f"r1{i}", 128, GB) for i in range(5)]
        wexp, wexpT = sb("wexp", 128, GB, E0), wk[9][0:8, :]
        v2 = sb("v2", 128, GB, H2, DH2 + 1)
        den2 = sb("den2", 128, GB, H2)
        csum, cbc = sb("csum", 128, GB), rows(wk[11])
        sel = sb("sel", 128, GB, E1)
        logit1, sel1 = sb("logit1", 128, G, GB, E1), sb("sel1", 128, G + 1, GB, E1)
        router_sum = sb("router_sum", 128, 2, E1)
        wmean = sb("wmean", 8, 4)
        selT, sel2b = sb("selT", 8, W, dtype=bf16), sb("sel2b", 8, PAIRS, 128, dtype=bf16)
        wmean_row = sb("wmean_row", 128, PAIRS)

        loaded, loaded_first, tables, par_a, par_v = (sem(n) for n in (
            "loaded", "loaded_first", "tables", "par_a", "par_v"))
        in_x, in_ctx = sem("in_x"), sem("in_ctx")
        chain_v, chain_a = sem("chain_v"), sem("chain_a")
        q_proj, k_proj, v_proj = sem("q_proj"), sem("k_proj"), sem("v_proj")
        q_parts, k_parts, qk_rot = sem("q_parts"), sem("k_parts"), sem("qk_rot")
        squares, norms, norms_sb, diag_done = sem("squares"), sem("norms"), sem("norms_sb"), sem("diag_done")
        v_sb, score, maha, log_done = sem("v_sb"), sem("score"), sem("maha"), sem("log_done")
        logits, exped, prob, prob_T, prob_T_sb = (sem(n) for n in
                                                  ("logits", "exped", "prob", "prob_T", "prob_T_sb"))
        fold, fold_sb, sums_inv, head_out = (sem(n) for n in ("fold", "fold_sb", "sums_inv", "head_out"))
        ln_stats, ln_rstd, ln_out, act_tr, act_T_sb = (sem(n) for n in
                                                       ("ln_stats", "ln_rstd", "ln_out", "act_tr", "act_T_sb"))
        gates, gate_v, gate_a, gate_rows, gate_T, gate_aT, gate_eM = (sem(n) for n in (
            "gates", "gate_v", "gate_a", "gate_rows", "gate_T", "gate_aT", "gate_eM"))
        gate_max, gate_tot = sem("gate_max"), sem("gate_tot")
        mx_bc, arg_done, dmat, ctx_masked, qk1, c_done, num = (sem(n) for n in (
            "mx_bc", "arg_done", "dmat", "ctx_masked", "qk1", "c_done", "num"))
        rt_logit, rt_v, rt_a, rt_w, rt_wT, rt_wT_sb, rt_bias, xb_done = (sem(n) for n in (
            "rt_logit", "rt_v", "rt_a", "rt_w", "rt_wT", "rt_wT_sb", "rt_bias", "xb_done"))
        up, gelu, down, moe_acc = sem("up"), sem("gelu"), sem("down"), sem("moe_acc")
        qkv2, q2_sb, kv2_sb, k2_masked, s2, z2, p2, pT2, pT2_sb, o2 = (sem(n) for n in (
            "qkv2", "q2_sb", "kv2_sb", "k2_masked", "s2", "z2", "p2", "pT2", "pT2_sb", "o2"))
        o2_row, o2_tr, o2_T, y2, y3, ctx_mean = (sem(n) for n in ("o2_row", "o2_tr", "o2_T", "y2", "y3", "ctx_mean"))
        rl_logit, rl_v, rl_a, stored = (sem(n) for n in ("rl_logit", "rl_v", "rl_a", "stored"))
        sel_here, mean_rows, sum_read = sem("sel_here"), sem("mean_rows"), sem("sum_read")
        in_bias, gate_proj = sem("in_bias"), sem("gate_proj")
        in2_all = 16 * (len(phase2) + 4)
        tot, sums_done, in2, selT_ps, selT_sb = (sem(n) for n in ("tot", "sums_done", "in2", "selT_ps", "selT_sb"))
        gup, silu, h_done, y4, f_stats, f_rstd, f_out, out_done = (sem(n) for n in (
            "gup", "silu", "h_done", "y4", "f_stats", "f_rstd", "f_out", "out_done"))

        block = ctx.enter_context(nc.Block())

        @block.sync
        def _(sp):
            for name in for_tables:
                sp.dma_start(res[name][:], a[name]).then_inc(loaded_first, 16)
            for name in rest:
                sp.dma_start(res[name][:], a[name]).then_inc(loaded, 16)
            sp.sem_inc(stored, 16)
            sp.sem_inc(out_done, 16)
            def group_of(name, g):
                return a[name][bass.ds(g, 1)].rearrange("g p n -> (g p) n")

            def load_context(g):
                sp.wait_ge(stored, g * 32 + 16)
                sp.wait_ge(ln_out, g * LNS + 1)
                sp.dma_start(ctx_T[:], group_of("ctx_T", g)).then_inc(in_ctx, 16)
                sp.dma_start(wk[23][:], group_of("ctx_row", g)).then_inc(in_ctx, 16)

            with sp.Fori(0, G - 1) as g:
                load_context(g)
                sp.wait_ge(act_T_sb, g * 5 + 5)
                sp.dma_start(x5_scratch[bass.ds(g, 1)].rearrange("g p n -> (g p) n"),
                             act_row[0][:].rearrange("p b d -> p (b d)")).then_inc(stored, 16)
                sp.dma_start(x5T_scratch[bass.ds(g, 1)].rearrange("g p n -> (g p) n"),
                             act_T[:]).then_inc(stored, 16)
            g = G - 1
            load_context(g)
            sp.wait_ge(ln_out, g * LNS + 2)
            for name in phase2:
                sp.dma_start(late[name], a[name]).then_inc(in2, 16)
            sp.dma_start(x5T_all[:, 0:g], x5T_scratch[0:g].rearrange("g p n -> p g n")).then_inc(in2, 16)
            sp.dma_start(x5_all[:, 0:g], x5_scratch[0:g].rearrange("g p n -> p g n")).then_inc(in2, 16)
            sp.wait_ge(act_T_sb, g * 5 + 5)
            sp.dma_start(x5T_all[:, g], act_T[:]).then_inc(in2, 16)
            sp.dma_start(x5_all[:, g], act_row[0][:].rearrange("p b d -> p (b d)")).then_inc(in2, 16)
            with sp.Fori(0, G) as g:
                sp.wait_ge(f_out, g + 2)
                sp.dma_start(out[bass.ds(g, 1)].rearrange("g b t d -> t (g b) d"),
                             act_row[0][:]).then_inc(out_done, 16)
            sp.wait_ge(out_done, 16 * G + 16)

        @block.vector
        def _(dve):
            v = nc.vector
            count = [0]

            def link(ins):
                count[0] += 1
                ins.then_inc(chain_v, 1)
                dve.wait_ge(chain_v, count[0])

            def restart():
                dve.sem_clear(chain_v)
                count[0] = 0

            restart()
            dve.wait_ge(loaded_first, 16 * len(for_tables))

            v.scalar_tensor_tensor(p_abs[:], par[:, 0:64], -1.0, par[:, 0:64], ALU.mult, ALU.min).then_inc(par_v, 1)
            dve.wait_ge(par_a, 1)
            link(v.scalar_tensor_tensor(p_sp[:], par[:, 0:64], 0.0, p_abs[:], ALU.max, ALU.add))
            dve.wait_ge(par_a, 2)
            link(v.tensor_scalar(p_sig[:], p_sig[:], 1.0, None, ALU.add))
            link(v.reciprocal(p_sig[:], p_sig[:]))
            sig, eta, gam, nu = (p_sp[:, 16 * i:16 * i + 16] for i in range(4))
            tau = par[:, 64:80]
            mu = p_sig[:, 0:H0]
            neg_mu, coef, amp, neg_amp, base, rmu, rnu = (p_col[:, i, :] for i in range(7))
            link(v.tensor_scalar(mu, mu, 1.0e-4, None, ALU.add))
            v.tensor_scalar(neg_mu, mu, -1.0, None, ALU.mult)
            link(v.reciprocal(rmu, mu))
            link(v.scalar_tensor_tensor(amp, sig, 0.5, rmu, ALU.mult, ALU.mult))
            v.tensor_scalar(neg_amp, amp, -1.0, None, ALU.mult)
            link(v.tensor_tensor(base, eta, gam, ALU.add))
            link(v.tensor_tensor(base, base, amp, ALU.add))
            link(v.scalar_tensor_tensor(coef, nu, float(DH0), tau, ALU.add, ALU.mult))
            link(v.tensor_scalar(coef, coef, -0.5, None, ALU.mult))
            sc = DH2 ** -0.5
            link(v.tensor_scalar(q_scale[:], p_sig[:, H0:H0 + 1], -sc, None, ALU.mult))
            link(v.tensor_tensor(q_scale[:], q_scale[:], top_rows, ALU.mult))
            link(v.scalar_tensor_tensor(q_scale[:], low_rows, sc, q_scale[:], ALU.mult, ALU.add))

            for h in range(H0):
                last = v.tensor_scalar(dec[:, h], dist[:], neg_mu[:, h:h + 1], -30.0, ALU.mult, ALU.max)
            last.then_inc(par_v, 1)

            MAGIC, C1, C2 = 12582912.0, 6.28125, 0.0019350051879882812
            C3 = 2 * math.pi - C1 - C2
            PI = 3.1415925
            for h in range(H0):
                last = v.tensor_scalar(ang[:, h], tramp[:], res["freq"][:, h:h + 1], None, ALU.mult)
            link(last)

            dve.wait_ge(par_a, 3)
            link(v.tensor_tensor(bias_t[:], dec[:], dec_inv[:], ALU.mult))
            link(v.tensor_scalar(bias_t[:], bias_t[:], -1.0, 2.0, ALU.mult, ALU.add))
            link(v.tensor_tensor(dec_inv[:], dec_inv[:], bias_t[:], ALU.mult))
            link(v.tensor_tensor(bias_t[:], dec[:], dec[:], ALU.mult))
            for h in range(H0):
                last = v.tensor_scalar(bias_t[:, h], bias_t[:, h], neg_amp[:, h:h + 1], base[:, h:h + 1],
                                       ALU.mult, ALU.add)
            last.then_inc(par_v, 1)

            link(v.tensor_scalar(turns, ang, 1 / (2 * math.pi), MAGIC, ALU.mult, ALU.add))
            link(v.tensor_scalar(turns, turns, -MAGIC, None, ALU.add))
            link(v.scalar_tensor_tensor(red, turns, -C1, ang, ALU.mult, ALU.add))
            link(v.scalar_tensor_tensor(red, turns, -C2, red, ALU.mult, ALU.add))
            link(v.scalar_tensor_tensor(red, turns, -C3, red, ALU.mult, ALU.add))
            link(v.tensor_scalar(red, red, PI, -PI, ALU.min, ALU.max))
            v.tensor_scalar(turns, red, math.pi / 2, -2 * math.pi, ALU.is_gt, ALU.mult).then_inc(par_v, 1)
            dve.wait_ge(par_v, 4)
            link(v.scalar_tensor_tensor(turns, red, math.pi / 2, turns, ALU.add, ALU.add))
            v.tensor_scalar(turns, turns, PI, -PI, ALU.min, ALU.max).then_inc(par_v, 1)

            link(v.reciprocal(rnu, nu))
            link(v.tensor_scalar(rnu, rnu, -2.0, None, ALU.mult))
            v.memset(v1[:], 1.0)
            v.memset(m_parts[:], 0.0)
            v.memset(v2[:], 1.0)
            v.memset(sel1[:, G], 0.0)
            v.memset(gate[6][:], 1.0)
            dve.wait_ge(par_a, 4)
            for h in range(H0):
                last = v.scalar_tensor_tensor(wgt[:, h], dec[:, h], rnu[:, h:h + 1], wgt[:, h], ALU.mult, ALU.mult)
            link(last)
            mask_b = mask_ij[:].unsqueeze(1).broadcast_to([128, H0, N])
            link(v.scalar_tensor_tensor(bias_t[:], bias_t[:], -0.5 * DH0, mask_b, ALU.mult, ALU.add))
            dve.wait_ge(loaded, 16 * len(rest))
            v.tensor_copy(sel24[:], res["sel24"])
            v.tensor_tensor(res["gate_w"][:, 1], res["gate_w"][:, 1], res["gate_w"][:, 2], ALU.add)
            dve.wait_ge(par_a, 6)
            v.tensor_scalar(sinT[:], sinT[:], sgn, None, ALU.mult).then_inc(tables, 1)
            dve.wait_ge(tables, 1)
            dve.sem_inc(ln_out, 1)

            def norm(g, i, src, dst, stats=ln_stats, rs=ln_rstd, per=LNS, done=None):
                for b in range(GB):
                    last = v.bn_stats(st[:, b, :], src[:, b])
                link(last)
                for b in range(GB):
                    last = v.bn_aggr(mv[:, b, :], st[:, b, :])
                last.then_inc(stats, 1)
                dve.wait_ge(rs, g * per + i + 1)
                for b in range(GB):
                    last = v.tensor_scalar(dst[:, b], src[:, b], mv[:, b, 0:1], rstd[:, b:b + 1],
                                           ALU.subtract, ALU.mult)
                last.then_inc(done, 1)

            def bc(m):
                return m.unsqueeze(2).broadcast_to([128, m.shape[1], 8])

            def top2(p, oh1, oh2, m1, m2, t, r):
                rk = rank.unsqueeze(1).broadcast_to([128, m1.shape[1], 8])
                for oh, m in ((oh1, m1), (oh2, m2)):
                    q = p if oh is oh1 else t
                    link(v.tensor_reduce(m, q, X, ALU.max))
                    link(v.tensor_tensor(oh, q, bc(m), ALU.is_equal))
                    link(v.tensor_tensor(oh, oh, rk, ALU.mult))
                    link(v.tensor_reduce(r, oh, X, ALU.max))
                    link(v.tensor_tensor(oh, rk, bc(r), ALU.is_equal))
                    if oh is oh1:
                        link(v.scalar_tensor_tensor(t, oh, -4.0, p, ALU.mult, ALU.add))

            with dve.Fori(0, G) as g:
                restart()
                bc_h = lambda t, h: t[:, h].unsqueeze(1).broadcast_to([128, GB, N])
                half = ((slice(0, DH0), slice(DH0, 128)), (slice(DH0, 128), slice(0, DH0)))
                for s in range(H0 + 5):
                    h = s - 5
                    if 0 <= h < H0:
                        dve.wait_ge(exped, g * H0 + h + 1)
                        if h >= 2:
                            dve.wait_ge(prob, g * H0 + h - 1)
                        v.reciprocal(rsum[:, h % 2, :], esum[:, h % 4, :]).then_inc(sums_inv, 1)
                    if s < H0:
                        for i, sm, dn in ((0, q_proj, q_parts), (2, k_proj, k_parts)):
                            src = bank[i // 2]
                            if s > 0:
                                dve.wait_ge(qk_rot, g * 2 * H0 + 2 * s - 1 + i // 2)
                            dve.wait_ge(sm, g * H0 + s + 1)
                            v.tensor_tensor(rows(wk[i]), rows(src), bc_h(cosT, s), ALU.mult)
                            for o, p in half:
                                last = v.tensor_tensor(rows(wk[i + 1][o]), rows(src[p]),
                                                       sinT[o, s].unsqueeze(1).broadcast_to([DH0, GB, N]), ALU.mult)
                            last.then_inc(dn, 1)
                    h = s - 2
                    if 0 <= h < H0:
                        M = rows(wk[(11, 21)[h % 2]])
                        dve.wait_ge(norms_sb, g * H0 + h + 1)
                        dve.wait_ge(score, g * H0 + h + 1)
                        for b in range(GB):
                            last = v.scalar_tensor_tensor(M[:, b], dec_inv[:, h], nrm[:, h % 2, 4 + b:5 + b],
                                                          rows(bank[4 + h % 2])[:, b], ALU.mult, ALU.add)
                        link(last)
                        v.scalar_tensor_tensor(M, M, 0.0, bc_h(wgt, h), ALU.min, ALU.mult).then_inc(maha, 1)
                    h = s - 3
                    if 0 <= h < H0:
                        dve.wait_ge(log_done, g * H0 + h + 1)
                        if h > 0:
                            dve.wait_ge(exped, g * H0 + h)
                        link(v.scalar_tensor_tensor(rows(wk[12]), rows(wk[(11, 21)[h % 2]]), coef[:, h:h + 1],
                                                    bc_h(bias_t, h), ALU.mult, ALU.add))
                        v.tensor_reduce(negmax[:, h % 2, :], rows(wk[12]), X, ALU.max,
                                        negate=True).then_inc(logits, 1)
                dve.wait_ge(head_out, g * H0 + H0)
                link(v.tensor_tensor(resid, rows(bank[7]), x_row[:], ALU.add))
                dve.wait_ge(in_ctx, g * 32 + 32)
                norm(g, 0, resid, act_row[0], done=ln_out)

                nabs, e_g, logf, csum_f, a_g, m_g, one = gate
                b_i, b_f = res["gate_b"][0:8, :], res["gate_b"][32:40, :]
                v.tensor_copy(v1[:, :, :, 0:DH1], wk[23][:].rearrange("p (b h d) -> p b h d", b=GB, h=H1))
                dve.wait_ge(gates, g + 1)
                link(v.tensor_scalar(logf[:], bank[0][32:40, :], b_f, None, ALU.add))
                v.scalar_tensor_tensor(nabs[:], logf[:], -1.0, logf[:], ALU.mult, ALU.min).then_inc(gate_v, 1)
                dve.wait_ge(gate_a, g + 1)
                link(v.scalar_tensor_tensor(logf[:], logf[:], 0.0, e_g[:], ALU.min, ALU.subtract))
                for b in range(GB):
                    c = slice(b * N, b * N + N)
                    last = v.tensor_tensor_scan(csum_f[:, c], one[:, c], logf[:, c], 0.0, ALU.mult, ALU.add)
                link(last)
                v.scalar_tensor_tensor(a_g[:], bank[0][0:8, :], b_i, csum_f[:], ALU.add,
                                       ALU.subtract).then_inc(gate_rows, 1)
                dve.wait_ge(gate_rows, g + 1)
                for b in range(GB):
                    c = slice(b * N, b * N + N)
                    last = v.tensor_tensor_scan(m_g[:, c], one[:, c], a_g[:, c], -3.0e38, ALU.mult, ALU.max)
                link(last)
                link(v.tensor_copy(m_parts[0:8, :], m_g[:]))
                link(v.tensor_tensor(logf[:], m_g[:], m_parts[0:8, :], ALU.subtract))
                link(v.tensor_copy(m_parts[32:40, :], logf[:]))
                v.tensor_tensor(m_parts[64:72, :], logf[:], m_parts[32:40, :], ALU.subtract).then_inc(gate_max, 1)
                v.tensor_tensor(csum_f[:], csum_f[:], m_g[:], ALU.add).then_inc(gate_tot, 1)
                dve.wait_ge(gate_aT, g + 1)
                link(v.tensor_copy(aT[:].rearrange("p b h -> p (b h)"), bank[2][:, 0:GB * H1]))
                for s in range(H1 + 1):
                    if s < H1:
                        dve.wait_ge(mx_bc, g * H1 + s + 1)
                        if s >= 2:
                            dve.wait_ge(c_done, g * H1 + s - 1)
                        for b in range(GB):
                            last = v.scalar_tensor_tensor(rows(wk[s % 2])[:, b], rows(bank[4 + s % 2])[:, b],
                                                          aT[:, b, s:s + 1], mask_ji[:], ALU.add, ALU.add)
                        last.then_inc(arg_done, 1)
                    h = s - 1
                    if h >= 0:
                        dve.wait_ge(dmat, g * H1 + h + 1)
                        dve.wait_ge(qk1, g * H1 + h + 1)
                        if h >= 2:
                            dve.wait_ge(num, g * H1 + h - 1)
                        v.tensor_tensor(wk[4 + h % 2][:], bank[6 + h % 2][:], wk[h % 2][:],
                                        ALU.mult).then_inc(c_done, 1)
                dve.wait_ge(num, g * H1 + H1)
                dve.wait_ge(gate_eM, g + 1)
                nv = [bank[2 + i][:, 0:2 * H1 * (DH1 + 1)].rearrange("p (b h d) -> p b h d", b=2, h=H1)
                      for i in range(2)]
                for i in range(2):
                    last = v.tensor_copy(den[:, 2 * i:2 * i + 2], nv[i][:, :, :, DH1])
                link(last)
                link(v.scalar_tensor_tensor(rden[:], den[:], -1.0, den[:], ALU.mult, ALU.max))
                link(v.tensor_tensor(den[:], rden[:], eM[:], ALU.max))
                link(v.tensor_scalar(den[:], den[:], 1.0e-6, None, ALU.add))
                link(v.reciprocal(rden[:], den[:]))
                hr = act_row[1][:].rearrange("p b (h d) -> p b h d", h=H1)
                for i in range(2):
                    last = v.tensor_tensor(hr[:, 2 * i:2 * i + 2], nv[i][:, :, :, 0:DH1],
                                           rden[:, 2 * i:2 * i + 2].unsqueeze(3).broadcast_to([128, 2, H1, DH1]),
                                           ALU.mult)
                link(last)
                norm(g, 1, act_row[1], resid, done=ln_out)
                dve.wait_ge(ln_out, g * LNS + 3)
                link(v.tensor_tensor(resid, resid, res["ln_scale"][:].unsqueeze(1).broadcast_to([128, GB, D]),
                                     ALU.mult))
                link(v.tensor_tensor(resid, resid, act_row[0][:], ALU.add))
                norm(g, 2, resid, act_row[1], done=ln_out)

                link(v.tensor_reduce(csum[:], rows(ctx_T), X, ALU.add))
                v.tensor_scalar(cbc[:], csum[:].unsqueeze(2).broadcast_to([128, GB, N]), 1.0 / N, None,
                                ALU.mult).then_inc(ctx_mean, 1)
                pr, oh1, oh2, t, ex = (r[:] for r in rt)
                m1, m2, r, ssum, rs = (q[:] for q in r1)
                dve.wait_ge(rt_logit, g + 1)
                link(v.tensor_tensor(pr, bank[7][:, 0:32].rearrange("p (b e) -> p b e", b=GB),
                                     res["gate_b0"][:].unsqueeze(1).broadcast_to([128, GB, E0]), ALU.add))
                link(v.tensor_reduce(m1, pr, X, ALU.max))
                v.tensor_tensor(t, pr, bc(m1), ALU.subtract).then_inc(rt_v, 1)
                dve.wait_ge(rt_a, g + 1)
                link(v.tensor_reduce(ssum, ex, X, ALU.add))
                link(v.reciprocal(rs, ssum))
                link(v.tensor_tensor(pr, ex, bc(rs), ALU.mult))
                top2(pr, oh1, oh2, m1, m2, t, r)
                link(v.tensor_tensor(ssum, m1, m2, ALU.add))
                link(v.tensor_scalar(ssum, ssum, 1.0e-9, None, ALU.add))
                link(v.reciprocal(rs, ssum))
                link(v.tensor_tensor(oh1, oh1, bc(m1), ALU.mult))
                link(v.tensor_tensor(oh2, oh2, bc(m2), ALU.mult))
                link(v.tensor_tensor(oh1, oh1, oh2, ALU.add))
                v.tensor_tensor(wexp[:], oh1, bc(rs), ALU.mult).then_inc(rt_w, 1)
                dve.wait_ge(rt_w, g + 1)
                acc = resid
                for e in range(E0S):
                    if e == 1:
                        dve.wait_ge(rt_wT, g + 1)
                        v.tensor_copy(wexpT[:], bank[6][0:8, :]).then_inc(rt_wT_sb, 1)
                    if e == 2:
                        dve.wait_ge(rt_bias, g + 1)
                        link(v.tensor_tensor(acc[:], rows(bank[7]), acc[:], ALU.add))
                    dve.wait_ge(down, g * E0S + e + 1)
                    y = rows(bank[4 + e % 2])
                    if e == 0:
                        dve.wait_ge(xb_done, g * 2 + 2)
                        v.tensor_tensor(acc[:], y, rows(wk[10]), ALU.add).then_inc(moe_acc, 1)
                    else:
                        for b in range(GB):
                            last = v.scalar_tensor_tensor(acc[:, b], y[:, b], wexp[:, b, e - 1:e], acc[:, b],
                                                          ALU.mult, ALU.add)
                        last.then_inc(moe_acc, 1)
                    dve.wait_ge(moe_acc, g * E0S + e + 1)
                norm(g, 3, resid, act_row[0], done=ln_out)

                dve.wait_ge(qkv2, g * 3 + 2)
                v.tensor_scalar(wk[0][:], bank[0][:], q_scale[:], None, ALU.mult).then_inc(q2_sb, 1)
                for s in range(H2):
                    dve.wait_ge(s2, g * H2 + s + 1)
                    S = rows(bank[4 + s % 2])
                    link(v.tensor_reduce(negmax[:, s % 2, :], S, X, ALU.max, negate=True))
                    if s >= 3:
                        dve.wait_ge(pT2, g * H2 + s - 2)
                    v.tensor_tensor(rows(wk[4 + s % 3]), S, negmax[:, s % 2, :].unsqueeze(2)
                                    .broadcast_to([128, GB, N]), ALU.add).then_inc(z2, 1)
                dve.wait_ge(o2, g * H2 + H2)
                ov = [bank[6 + i][:, 0:2 * H2 * (DH2 + 1)].rearrange("p (b h d) -> p b h d", b=2, h=H2)
                      for i in range(2)]
                for i in range(2):
                    last = v.reciprocal(den2[:, 2 * i:2 * i + 2], ov[i][:, :, :, DH2])
                link(last)
                orow = rows(wk[9]).rearrange("p b (h d) -> p b h d", h=H2)
                for i in range(2):
                    last = v.tensor_tensor(orow[:, 2 * i:2 * i + 2], ov[i][:, :, :, 0:DH2],
                                           den2[:, 2 * i:2 * i + 2].unsqueeze(3).broadcast_to([128, 2, H2, DH2]),
                                           ALU.mult)
                last.then_inc(o2_row, 1)
                dve.wait_ge(y2, g + 1)
                dve.wait_ge(in_bias, g * 2 + 1)
                link(v.tensor_tensor(resid, rows(bank[3]), rows(wk[12]), ALU.add))
                norm(g, 4, resid, act_row[1], done=ln_out)
                dve.wait_ge(y3, g + 1)
                dve.wait_ge(in_bias, g * 2 + 2)
                link(v.tensor_tensor(resid, rows(bank[1]), rows(wk[13]), ALU.add))
                norm(g, 5, resid, act_row[0], done=ln_out)

                dve.wait_ge(rl_logit, g + 1)
                v.tensor_tensor(logit1[:, bass.ds(g, 1)].rearrange("p g b e -> p (g b) e"),
                                bank[3][:, 0:GB * E1].rearrange("p (b e) -> p b e", b=GB),
                                res["lb_bias"][:].unsqueeze(1).broadcast_to([128, GB, E1]),
                                ALU.add).then_inc(rl_v, 1)

            restart()
            dve.wait_ge(rl_a, 1)
            by_expert = [work[:, i * B * E1:(i + 1) * B * E1].rearrange("p (b e) -> p b e", b=B) for i in range(5)]
            ex, pr, oh1, oh2, t = by_expert
            m1, m2, r, ssum, rs = (wk[5][:, i * B:(i + 1) * B] for i in range(5))
            link(v.tensor_scalar(ex, ex, 1.0, None, ALU.add))
            link(v.reciprocal(pr, ex))
            top2(pr, oh1, oh2, m1, m2, t, r)
            link(v.tensor_tensor(ssum, m1, m2, ALU.add))
            link(v.tensor_scalar(ssum, ssum, 1.0e-8, None, ALU.add))
            link(v.reciprocal(rs, ssum))
            link(v.tensor_tensor(sel1[:, 0:G].rearrange("p g b e -> p (g b) e"), oh1, oh2, ALU.add))
            link(v.tensor_tensor(oh1, oh1, bc(m1), ALU.mult))
            link(v.tensor_tensor(oh2, oh2, bc(m2), ALU.mult))
            link(v.tensor_tensor(oh1, oh1, oh2, ALU.add))
            link(v.tensor_tensor(oh1, oh1, bc(rs), ALU.mult))
            v.tensor_reduce(router_sum[:, 0], sel1[:, 0:G].rearrange("p g b e -> p e (g b)"), X, ALU.add)
            v.tensor_reduce(router_sum[:, 1], oh1.rearrange("p b e -> p e b"), X, ALU.add).then_inc(sums_done, 1)

            restart()
            dve.wait_ge(tot, 1)
            link(v.tensor_copy(wmean[:, 0:2], bank[0][0:8, 0:2]))
            link(v.tensor_scalar(wmean[:, 0:1], wmean[:, 0:1], 1.0, None, ALU.max))
            link(v.reciprocal(wmean[:, 2:3], wmean[:, 0:1]))
            v.tensor_tensor(wmean[:, 3:4], wmean[:, 1:2], wmean[:, 2:3], ALU.mult).then_inc(f_out, 1)
            dve.wait_ge(in2, in2_all)
            v.tensor_copy(sel2b[:], late["sel2"])
            dve.wait_ge(mean_rows, 1)
            link(v.tensor_copy(wmean_row[:], bank[0][:, 0:PAIRS]))
            for p in range(PAIRS):
                last = v.tensor_scalar(late["w_d1"][:, p], late["w_d1"][:, p], wmean_row[:, p:p + 1], None, ALU.mult)
            last.then_inc(h_done, 1)
            dve.sem_inc(sum_read, 1)
            with dve.Fori(0, G) as g:
                restart()
                for p in range(BLK):
                    dve.wait_ge(silu, g * BLK + p + 1)
                    dve.wait_ge(gup, g * BLK + p + 1)
                    hid = wk[2 + p]
                    if p < PAIRS:
                        link(v.tensor_tensor(hid[:], bank[2 + p % 2][:], wk[p % 2][:], ALU.mult))
                        v.tensor_tensor(hid[:], bank[4 + p % 2][:], hid[:], ALU.mult).then_inc(h_done, 1)
                    else:
                        v.tensor_tensor(hid[:], bank[2 + p % 2][:], wk[p % 2][:], ALU.mult).then_inc(h_done, 1)
                dve.wait_ge(y4, g + 1)
                x5 = x5_all[:, bass.ds(g, 1)].rearrange("p g (b d) -> p (g b) d", b=GB)
                v.tensor_tensor(resid, rows(bank[7]), x5, ALU.add).then_inc(sum_read, 1)
                dve.wait_ge(sum_read, g + 2)
                dve.wait_ge(out_done, g * 16 + 16)
                norm(g, 0, resid, act_row[0], f_stats, f_rstd, 1, f_out)

        @block.scalar
        def _(act):
            count = [0]

            def link(ins):
                count[0] += 1
                ins.then_inc(chain_a, 1)
                act.wait_ge(chain_a, count[0])

            def restart():
                act.sem_clear(chain_a)
                count[0] = 0

            def fn(o, i, f, **k):
                return nc.scalar.activation(o, i, f, **k)

            restart()
            act.preload_act_table_set("natural_log_exp_and_others")
            act.wait_ge(par_v, 1)
            link(fn(p_abs[:], p_abs[:], ACT.Exp))
            fn(p_abs[:], p_abs[:], ACT.Ln, bias=1.0).then_inc(par_a, 1)
            fn(p_sig[:], par[:, 80:97], ACT.Exp, scale=-1.0).then_inc(par_a, 1)
            act.wait_ge(par_v, 2)
            link(fn(dec_inv[:], dec[:], ACT.Exp, scale=-1.0))
            fn(dec[:], dec[:], ACT.Exp).then_inc(par_a, 1)
            act.wait_ge(par_v, 3)
            link(fn(bias_t[:], bias_t[:], ACT.Ln))
            fn(wgt[:], bias_t[:], ACT.Exp, scale=-1.0).then_inc(par_a, 1)
            act.wait_ge(par_v, 4)
            fn(sinT[:], red, ACT.Sin).then_inc(par_a, 1)
            act.wait_ge(par_v, 5)
            fn(cosT[:], turns, ACT.Sin).then_inc(par_a, 1)
            act.preload_act_table_set("natural_log_exp_and_others")
            for c in range(4):
                act.wait_ge(fold, c + 1)
                fn(vo[:, 4 * c:4 * c + 4].rearrange("p h d -> p (h d)"), bank[c][:], ACT.Copy).then_inc(fold_sb, 1)

            def norm(g, i, stats=ln_stats, rs=ln_rstd, per=LNS):
                act.wait_ge(stats, g * per + i + 1)
                link(fn(ln_t[:], mv[:, :, 1], ACT.Ln, bias=res["cols"][:, 5:6]))
                fn(rstd[:], ln_t[:], ACT.Exp, scale=-0.5).then_inc(rs, 1)

            def to_T(g, i, src_bank):
                act.wait_ge(act_tr, g * 5 + i + 1)
                fn(act_T[:], src_bank[:], ACT.Copy).then_inc(act_T_sb, 1)

            with act.Fori(0, G) as g:
                restart()
                for s in range(H0 + 7):
                    h = s - 4
                    if 0 <= h < H0:
                        act.wait_ge(logits, g * H0 + h + 1)
                        if h >= 3:
                            act.wait_ge(prob_T, g * H0 + h - 2)
                        P = rows(wk[13 + h % 3])
                        for b in range(GB):
                            last = fn(P[:, b], rows(wk[12])[:, b], ACT.Exp, bias=negmax[:, h % 2, b:b + 1],
                                      accum_out=esum[:, h % 4, b:b + 1])
                        last.then_inc(exped, 1)
                    h = s - 1
                    if 0 <= h < H0:
                        act.wait_ge(qk_rot, g * 2 * H0 + 2 * h + 2)
                        fn(wk[8][:], wk[4 + h % 2][:], ACT.Square)
                        fn(wk[9][:], wk[6 + h % 2][:], ACT.Square).then_inc(squares, 1)
                    h = s - 5
                    if 0 <= h < H0:
                        act.wait_ge(v_proj, g * H0 + h + 1)
                        if h >= 3:
                            act.wait_ge(head_out, g * H0 + h - 2)
                        fn(wk[16 + h % 3][:], bank[2][:], ACT.Copy).then_inc(v_sb, 1)
                    h = s - 6
                    if 0 <= h < H0:
                        act.wait_ge(prob_T, g * H0 + h + 1)
                        if h >= 2:
                            act.wait_ge(head_out, g * H0 + h - 1)
                        fn(wk[19 + h % 2][:], bank[prob_T_bank(h)][:], ACT.Copy).then_inc(prob_T_sb, 1)
                    h = s - 1
                    if 0 <= h < H0:
                        act.wait_ge(norms, g * H0 + h + 1)
                        fn(nrm[:, h % 2, :], bank[3][:, 0:8], ACT.Copy).then_inc(norms_sb, 1)
                    h = s - 2
                    if 0 <= h < H0:
                        act.wait_ge(maha, g * H0 + h + 1)
                        fn(wk[(11, 21)[h % 2]][:], wk[(11, 21)[h % 2]][:], ACT.Ln, bias=1.0).then_inc(log_done, 1)
                norm(g, 0)
                to_T(g, 0, bank[4])
                act.wait_ge(gate_v, g + 1)
                link(fn(gate[1][:], gate[0][:], ACT.Exp))
                fn(gate[1][:], gate[1][:], ACT.Ln, bias=res["cols"][0:8, 6:7]).then_inc(gate_a, 1)
                for h in range(H1):
                    act.wait_ge(arg_done, g * H1 + h + 1)
                    fn(wk[h % 2][:], wk[h % 2][:], ACT.Exp).then_inc(dmat, 1)
                act.wait_ge(gate_T, g + 1)
                fn(eM[:].rearrange("p b h -> p (b h)"), bank[0][:, 0:GB * H1], ACT.Exp, scale=-1.0).then_inc(gate_eM, 1)
                norm(g, 1)
                norm(g, 2)
                to_T(g, 1, bank[6])
                act.wait_ge(rt_v, g + 1)
                fn(rt[4][:], rt[3][:], ACT.Exp).then_inc(rt_a, 1)
                for e in range(E0S):
                    for c in range(CH):
                        act.wait_ge(up, g * E0S * CH + e * CH + c + 1)
                        if e >= 2:
                            act.wait_ge(down, g * E0S + e - 1)
                        fn(wk[4 * (e % 2) + c][:], bank[c][:], ACT.Gelu_apprx_tanh,
                           bias=res["b_up"][:, e, c:c + 1]).then_inc(gelu, 1)
                act.preload_act_table_set("natural_log_exp_and_others")
                norm(g, 3)
                to_T(g, 2, bank[6])
                act.wait_ge(qkv2, g * 3 + 1)
                fn(wk[1][:], bank[1][:], ACT.Copy).then_inc(kv2_sb, 1)
                act.wait_ge(qkv2, g * 3 + 3)
                fn(v2[:, :, :, 0:DH2], bank[2][:].rearrange("p (b h d) -> p b h d", b=GB, h=H2),
                   ACT.Copy).then_inc(kv2_sb, 1)
                for s in range(H2 + 2):
                    if s < H2:
                        act.wait_ge(z2, g * H2 + s + 1)
                        fn(wk[4 + s % 3][:], wk[4 + s % 3][:], ACT.Exp).then_inc(p2, 1)
                    h = s - 2
                    if h >= 0:
                        act.wait_ge(pT2, g * H2 + h + 1)
                        if h >= 2:
                            act.wait_ge(o2, g * H2 + h - 1)
                        fn(wk[7 + h % 2][:], bank[2 + h % 2][:], ACT.Copy).then_inc(pT2_sb, 1)
                act.wait_ge(o2_tr, g + 1)
                fn(wk[10][:], bank[2][:], ACT.Copy).then_inc(o2_T, 1)
                norm(g, 4)
                to_T(g, 3, bank[0])
                norm(g, 5)
                to_T(g, 4, bank[2])

            act.wait_ge(rl_v, G)
            fn(work[:, 0:B * E1], logit1[:].rearrange("p g b e -> p (g b e)"), ACT.Exp, scale=-1.0).then_inc(rl_a, 1)

            act.wait_ge(selT_ps, 1)
            fn(selT[:], bank[6][0:8, :], ACT.Copy).then_inc(selT_sb, 1)
            with act.Fori(0, G) as g:
                restart()
                for p in range(BLK):
                    if p == PAIRS:
                        act.wait_ge(selT_ps, g + 2)
                        fn(selT[:], bank[6][0:8, :], ACT.Copy).then_inc(selT_sb, 1)
                    act.wait_ge(gate_proj, g * BLK + p + 1)
                    if p >= 2:
                        act.wait_ge(h_done, g * BLK + p)
                    fn(wk[p % 2][:], bank[p % 2][:], ACT.Silu).then_inc(silu, 1)
                act.preload_act_table_set("natural_log_exp_and_others")
                norm(g, 0, f_stats, f_rstd, 1)

        @block.gpsimd
        def _(pool):
            q = nc.gpsimd
            pool.wait_ge(loaded_first, 16 * len(for_tables))
            pool.wait_ge(loaded, 16 * len(rest))
            with pool.Fori(0, G) as g:
                for name, tile in (("x_T", x_T[:]), ("x_row", x_row[:].rearrange("p b d -> p (b d)"))):
                    q.dma_start(tile, a[name][bass.ds(g, 1)].rearrange("g p n -> (g p) n")).then_inc(in_x, 16)
                for s in range(H0 + 5):
                    if s < H0:
                        pool.wait_ge(q_parts, g * H0 + s + 1)
                        if s >= 2:
                            pool.wait_ge(score, g * H0 + s - 1)
                        q.tensor_tensor(wk[4 + s % 2][:], wk[0][:], wk[1][:], ALU.add).then_inc(qk_rot, 1)
                    h = s - 1
                    if 0 <= h < H0:
                        pool.wait_ge(norms_sb, g * H0 + h + 1)
                        if h >= 2:
                            pool.wait_ge(score, g * H0 + h - 1)
                        q.tensor_tensor(rows(wk[(22, 10)[h % 2]]), ident[:].unsqueeze(1).broadcast_to([128, GB, N]),
                                        nrm[:, h % 2, 0:4].unsqueeze(2).broadcast_to([128, GB, N]),
                                        ALU.mult).then_inc(diag_done, 1)
                    if s < H0:
                        pool.wait_ge(k_parts, g * H0 + s + 1)
                        q.tensor_tensor(wk[6 + s % 2][:], wk[2][:], wk[3][:], ALU.add).then_inc(qk_rot, 1)
                    h = s - 5
                    if 0 <= h < H0:
                        pool.wait_ge(sums_inv, g * H0 + h + 1)
                        P = rows(wk[13 + h % 3])
                        q.tensor_tensor(P, P, rsum[:, h % 2, :].unsqueeze(2).broadcast_to([128, GB, N]),
                                        ALU.mult).then_inc(prob, 1)
                pool.wait_ge(in_ctx, g * 32 + 32)
                for h in range(H1):
                    if h >= 2:
                        pool.wait_ge(qk1, g * H1 + h - 1)
                    q.tensor_tensor(wk[2 + h % 2][:], ctx_T[:], head_mask1[:, h:h + 1].broadcast_to([128, W]),
                                    ALU.mult).then_inc(ctx_masked, 1)
                pool.wait_ge(ln_out, g * LNS + 4)
                q.tensor_tensor(rows(wk[10]), act_row[1][:],
                                res["b_sh"][:].unsqueeze(1).broadcast_to([128, GB, D]), ALU.add).then_inc(xb_done, 1)
                pool.wait_ge(xb_done, g * 2 + 1)
                q.tensor_tensor(rows(wk[10]), rows(wk[10]), act_row[1][:], ALU.add).then_inc(xb_done, 1)
                for h in range(H2):
                    pool.wait_ge(kv2_sb, g * 2 + 1)
                    if h >= 2:
                        pool.wait_ge(s2, g * H2 + h - 1)
                    q.tensor_tensor(wk[2 + h % 2][:], wk[1][:], head_mask2[:, h:h + 1].broadcast_to([128, W]),
                                    ALU.mult).then_inc(k2_masked, 1)
                q.tensor_tensor(rows(wk[12]), act_row[0][:], res["bout"][:].unsqueeze(1).broadcast_to([128, GB, D]),
                                ALU.add).then_inc(in_bias, 1)
                pool.wait_ge(ln_out, g * LNS + 6)
                q.tensor_tensor(rows(wk[13]), act_row[1][:], res["xb"][:].unsqueeze(1).broadcast_to([128, GB, D]),
                                ALU.add).then_inc(in_bias, 1)
            pool.wait_ge(sums_done, 1)
            with pool.Fori(0, G + 1) as g:
                q.tensor_copy(sel[:], sel1[:, bass.ds(g, 1)].rearrange("p g b e -> p (g b) e")).then_inc(sel_here, 1)
                pool.wait_ge(selT_ps, g + 1)

        @block.tensor
        def _(pe):
            def mm(o, l, r, start=True, stop=True):
                return nc.tensor.matmul(o, l, r, start=start, stop=stop, skip_group_check=True)

            def transposes(dst, src, sem_out):
                for b in range(GB):
                    last = nc.tensor.transpose(rows(dst)[:, b], src[:, b], ident[:])
                last.then_inc(sem_out, 1)

            pe.wait_ge(loaded_first, 16 * len(for_tables))
            pe.wait_ge(loaded, 16 * len(rest))
            for c in range(4):
                for h in range(4 * c, 4 * c + 4):
                    last = mm(rows(bank[c])[:, h % 4], res["wvT0"][:, h], res["wo0"][:, h], start=h % 4 == 0)
                last.then_inc(fold, 1)
            pe.wait_ge(fold_sb, 4)
            with pe.Fori(0, G) as g:
                pe.wait_ge(in_x, g * 32 + 32)
                def scores_of(h, g=g):
                    pe.wait_ge(diag_done, g * H0 + h + 1)
                    if h >= 2:
                        pe.wait_ge(maha, g * H0 + h - 1)
                    S = bank[4 + h % 2]
                    mm(S[:], dec[:, h], wk[(22, 10)[h % 2]][:], stop=False)
                    for b in range(GB):
                        last = mm(rows(S)[:, b], rows(wk[4 + h % 2])[:, b], rows(wk[6 + h % 2])[:, b],
                                  start=False)
                    last.then_inc(score, 1)

                def values_of(h, g=g):
                    if h > 0:
                        pe.wait_ge(v_sb, g * H0 + h)
                    for b in range(GB):
                        last = mm(rows(bank[2])[:, b], rows(x_T)[:, b], vo[:, h], start=b == 0)
                    last.then_inc(v_proj, 1)

                def norms_of(h, g=g):
                    pe.wait_ge(squares, g * H0 + h + 1)
                    if h > 0:
                        pe.wait_ge(norms_sb, g * H0 + h)
                    for b in range(GB):
                        mm(bank[3][:, b:b + 1], rows(wk[9])[:, b], half_col, start=b == 0)
                        last = mm(bank[3][:, 4 + b:5 + b], rows(wk[8])[:, b], half_col, start=False)
                    last.then_inc(norms, 1)

                def transpose_probs(h, g=g):
                    pe.wait_ge(prob, g * H0 + h + 1)
                    if h < H0 - 2 and h > 0:
                        pe.wait_ge(prob_T_sb, g * H0 + h)
                    if h == H0 - 2:
                        pe.wait_ge(k_parts, g * H0 + H0)
                    transposes(bank[prob_T_bank(h)], rows(wk[13 + h % 3]), prob_T)

                def add_head(h, g=g):
                    pe.wait_ge(prob_T_sb, g * H0 + h + 1)
                    pe.wait_ge(v_sb, g * H0 + h + 1)
                    for b in range(GB):
                        last = mm(rows(bank[7])[:, b], rows(wk[19 + h % 2])[:, b], rows(wk[16 + h % 3])[:, b],
                                  start=h == 0 and b == 0, stop=h == H0 - 1)
                    last.then_inc(head_out, 1)

                for s in range(H0 + 7):
                    if s < H0:
                        if s > 0:
                            pe.wait_ge(q_parts, g * H0 + s)
                        mm(bank[0][:], res["wq0"][:, s], x_T[:]).then_inc(q_proj, 1)
                        if s > 0:
                            pe.wait_ge(k_parts, g * H0 + s)
                        mm(bank[1][:], res["wk0"][:, s], x_T[:]).then_inc(k_proj, 1)
                    tail = s >= H0
                    if tail and s - 1 < H0:
                        norms_of(s - 1)
                    if 0 <= s - 2 < H0:
                        scores_of(s - 2)
                    if tail and s - 6 < H0:
                        transpose_probs(s - 6)
                    if 0 <= s - 5 < H0:
                        values_of(s - 5)
                    if 0 <= s - 7:
                        add_head(s - 7)
                    if not tail and 0 <= s - 6:
                        transpose_probs(s - 6)
                    if not tail and 0 <= s - 1:
                        norms_of(s - 1)
                pe.wait_ge(in_ctx, g * 32 + 32)
                gw = res["gate_w"]
                mm(bank[0][0:40, :], gw[:, 1], ctx_T[:], stop=False)
                pe.wait_ge(ln_out, g * LNS + 2)
                transposes(bank[4], act_row[0], act_tr)
                pe.wait_ge(act_T_sb, g * 5 + 1)
                mm(bank[0][0:40, :], gw[:, 0], act_T[:], start=False).then_inc(gates, 1)

                def gate_columns(dst, src, sem_out):
                    for b in range(GB):
                        last = mm(dst[:, b * H1:b * H1 + H1], src[:, b * N:b * N + N], ident[0:8, 0:8], start=b == 0)
                    last.then_inc(sem_out, 1)
                pe.wait_ge(gate_rows, g + 1)
                gate_columns(bank[2], gate[4], gate_aT)
                nv = [bank[2 + i][:, 0:2 * H1 * (DH1 + 1)].rearrange("p (b h d) -> p b h d", b=2, h=H1)
                      for i in range(2)]
                for s in range(H1 + 2):
                    if s < H1:
                        if s >= 2:
                            pe.wait_ge(arg_done, g * H1 + s - 1)
                        else:
                            pe.wait_ge(gate_max, g + 1)
                        mm(bank[4 + s % 2][:], sel24[:, s], m_parts[:]).then_inc(mx_bc, 1)
                        pe.wait_ge(ctx_masked, g * H1 + s + 1)
                        if s >= 2:
                            pe.wait_ge(c_done, g * H1 + s - 1)
                        for b in range(GB):
                            last = mm(rows(bank[6 + s % 2])[:, b], rows(wk[2 + s % 2])[:, b], rows(act_T)[:, b],
                                      start=b == 0)
                        last.then_inc(qk1, 1)
                    if s == H1:
                        pe.wait_ge(gate_tot, g + 1)
                        gate_columns(bank[0], gate[3], gate_T)
                    h = s - 2
                    if h >= 0:
                        pe.wait_ge(c_done, g * H1 + h + 1)
                        for b in range(GB):
                            last = mm(nv[b // 2][:, b % 2, h, :], rows(wk[4 + h % 2])[:, b], v1[:, b, h, :],
                                      start=h == 0 and b % 2 == 0)
                        last.then_inc(num, 1)
                pe.wait_ge(ln_out, g * LNS + 4)
                transposes(bank[6], act_row[1], act_tr)
                pe.wait_ge(act_T_sb, g * 5 + 2)
                for b in range(GB):
                    last = mm(bank[7][:, b * E0:b * E0 + E0], rows(act_T)[:, b], res["gw0"][:], start=b == 0)
                last.then_inc(rt_logit, 1)
                for s in range(E0S + 1):
                    if s < E0S:
                        for c in range(CH):
                            if s > 0:
                                pe.wait_ge(gelu, g * E0S * CH + (s - 1) * CH + c + 1)
                            mm(bank[c][:], res["w_up"][:, s, c * 128:c * 128 + 128], act_T[:]).then_inc(up, 1)
                    e = s - 1
                    if e >= 0:
                        pe.wait_ge(gelu, g * E0S * CH + e * CH + CH)
                        if e >= 2:
                            pe.wait_ge(moe_acc, g * E0S + e - 1)
                        for b in range(GB):
                            for c in range(CH):
                                last = mm(rows(bank[4 + e % 2])[:, b], rows(wk[4 * (e % 2) + c])[:, b],
                                          res["w_down"][:, e, c], start=b == 0 and c == 0)
                        last.then_inc(down, 1)
                    if e == 0:
                        pe.wait_ge(rt_w, g + 1)
                        for b in range(GB):
                            last = nc.tensor.transpose(bank[6][0:8, b * N:b * N + N], wexp[:, b], ident[:])
                        last.then_inc(rt_wT, 1)
                    if e == 1:
                        pe.wait_ge(rt_wT_sb, g + 1)
                        for b in range(GB):
                            last = mm(rows(bank[7])[:, b], wexpT[:, b * N:b * N + N], res["b_down"][:],
                                      start=b == 0)
                        last.then_inc(rt_bias, 1)
                pe.wait_ge(ln_out, g * LNS + 5)
                transposes(bank[6], act_row[0], act_tr)
                pe.wait_ge(act_T_sb, g * 5 + 3)
                mm(bank[1][:], res["wk2"][:], act_T[:]).then_inc(qkv2, 1)
                mm(bank[0][:], res["wq2"][:], act_T[:]).then_inc(qkv2, 1)
                for b in range(GB):
                    last = mm(rows(bank[2])[:, b], rows(act_T)[:, b], res["wv2"][:], start=b == 0)
                last.then_inc(qkv2, 1)
                pe.wait_ge(q2_sb, g + 1)
                ov = [bank[6 + i][:, 0:2 * H2 * (DH2 + 1)].rearrange("p (b h d) -> p b h d", b=2, h=H2)
                      for i in range(2)]
                for s in range(H2 + 3):
                    if s < H2:
                        pe.wait_ge(k2_masked, g * H2 + s + 1)
                        if s >= 2:
                            pe.wait_ge(z2, g * H2 + s - 1)
                        for b in range(GB):
                            last = mm(rows(bank[4 + s % 2])[:, b], rows(wk[0])[:, b], rows(wk[2 + s % 2])[:, b],
                                      start=b == 0)
                        last.then_inc(s2, 1)
                    h = s - 2
                    if 0 <= h < H2:
                        pe.wait_ge(p2, g * H2 + h + 1)
                        if h >= 2:
                            pe.wait_ge(pT2_sb, g * H2 + h - 1)
                        else:
                            pe.wait_ge(kv2_sb, g * 2 + 2)
                        transposes(bank[2 + h % 2], rows(wk[4 + h % 3]), pT2)
                    h = s - 3
                    if h >= 0:
                        pe.wait_ge(pT2_sb, g * H2 + h + 1)
                        for b in range(GB):
                            last = mm(ov[b // 2][:, b % 2, h, :], rows(wk[7 + h % 2])[:, b], v2[:, b, h, :],
                                      start=h == 0 and b % 2 == 0)
                        last.then_inc(o2, 1)
                pe.wait_ge(o2_row, g + 1)
                transposes(bank[2], rows(wk[9]), o2_tr)
                pe.wait_ge(o2_T, g + 1)
                for b in range(GB):
                    last = mm(rows(bank[3])[:, b], rows(wk[10])[:, b], res["wout2"][:], start=b == 0)
                last.then_inc(y2, 1)
                pe.wait_ge(ctx_mean, g + 1)
                for b in range(GB):
                    mm(rows(bank[1])[:, b], cbc[:, b], res["w2x"][:], start=b == 0, stop=False)
                pe.wait_ge(ln_out, g * LNS + 6)
                transposes(bank[0], act_row[1], act_tr)
                pe.wait_ge(act_T_sb, g * 5 + 4)
                for b in range(GB):
                    last = mm(rows(bank[1])[:, b], rows(act_T)[:, b], res["w1x"][:], start=False)
                last.then_inc(y3, 1)
                pe.wait_ge(ln_out, g * LNS + 7)
                transposes(bank[2], act_row[0], act_tr)
                pe.wait_ge(act_T_sb, g * 5 + 5)
                for b in range(GB):
                    last = mm(bank[3][:, b * E1:b * E1 + E1], rows(act_T)[:, b], res["gw1"][:], start=b == 0)
                last.then_inc(rl_logit, 1)

            pe.wait_ge(sums_done, 1)
            mm(bank[0][0:8, 0:1], router_sum[:, 0], ones_col)
            mm(bank[0][0:8, 1:2], router_sum[:, 1], ones_col, start=False).then_inc(tot, 1)
            pe.wait_ge(in2, in2_all)
            pe.wait_ge(f_out, 1)
            for p in range(PAIRS):
                last = mm(bank[0][:, p:p + 1], late["sel2"][:, p], wmean[:, 3:4], start=p == 0)
            last.then_inc(mean_rows, 1)

            def transpose_choices(k):
                pe.wait_ge(sel_here, k)
                for b in range(GB):
                    last = nc.tensor.transpose(bank[6][0:8, b * N:b * N + N], sel[:, b], ident[:])
                last.then_inc(selT_ps, 1)
            transpose_choices(1)
            with pe.Fori(0, G) as g:
                x5T = x5T_all[:, bass.ds(g, 1)].rearrange("p g n -> p (g n)")
                for s in range(BLK + 1):
                    p = s
                    if p < BLK:
                        if p != 1:
                            pe.wait_ge(h_done, g * BLK + max(p, 1))
                        if p == PAIRS:
                            transpose_choices(g + 2)
                        mm(bank[p % 2][:], late["w_g1"][:, p], x5T).then_inc(gate_proj, 1)
                        last = mm(bank[2 + p % 2][:], late["w_u1"][:, p], x5T)
                        if p < PAIRS:
                            pe.wait_ge(selT_sb, g + 1)
                            last = mm(bank[4 + p % 2][:], sel2b[:, p], selT[:])
                        last.then_inc(gup, 1)
                    p = s - 1
                    if p >= 0:
                        pe.wait_ge(h_done, g * BLK + p + 2)
                        if p == 0:
                            pe.wait_ge(sum_read, g + 1)
                        for b in range(GB):
                            last = mm(rows(bank[7])[:, b], rows(wk[2 + p])[:, b], late["w_d1"][:, p],
                                      start=p == 0 and b == 0, stop=p == BLK - 1)
                last.then_inc(y4, 1)


def layouts(inp):
    import numpy as np
    f = {k: np.asarray(v) for k, v in inp.items()}
    c = np.ascontiguousarray

    def row_groups(x):
        return c(x.reshape(G, GB, N, D).transpose(0, 2, 1, 3).reshape(G, N, W))

    def T_groups(x):
        return c(x.reshape(G, GB, N, D).transpose(0, 3, 1, 2).reshape(G, D, W))

    def tile(v):
        return c(np.tile(v.reshape(1, -1), (128, 1)))

    def heads(w, parts):
        r = w.reshape(D, 2, H0, DH0)
        return c(np.stack([r[:, p] for p in parts], 2).reshape(D, H0, len(parts) * DH0))

    def spread(i_gate, f_gate, shape):
        r = np.zeros((40,) + shape[1:], i_gate.dtype)
        r[0:8], r[32:40] = i_gate.reshape(shape), f_gate.reshape(shape)
        return r

    i = np.arange(128)
    f32 = np.float32
    cols = np.zeros((128, 40), f32)
    cols[:, 0] = np.where((i < 64) == (i % 64 < 32), -1, 1)
    cols[:, 1], cols[:, 2] = i < H2T * DH2, i >= H2T * DH2
    cols[:, 3], cols[:, 4], cols[:, 5], cols[:, 6] = 1, -0.5, 1e-5, 1
    cols[:, 8:16] = (i[:, None] // DH1 == np.arange(H1)) * DH1 ** -0.5
    cols[:, 16:32] = i[:, None] // DH2 == np.arange(H2)
    cols[:, 32:40] = 8 - np.arange(8)
    e = np.arange(8)
    a = dict(
        x_row=row_groups(f["x"]), x_T=T_groups(f["x"]),
        ctx_row=row_groups(f["ctx_1024"]), ctx_T=T_groups(f["ctx_1024"]),
        ident=np.eye(128, dtype=f32),
        dist=np.abs(i[:, None] - i).astype(f32),
        mask_ij=np.where(i[:, None] >= i, 0, NEG).astype(f32),
        mask_ji=np.where(i[:, None] <= i, 0, NEG).astype(f32),
        tramp=c(np.tile(i.astype(f32), (128, 1))),
        cols=cols,
        par=tile(np.concatenate([f["L0_attn_" + k] for k in
                                 ("sigma_raw", "eta_raw", "gamma_raw", "nu_raw", "tau", "mu_raw")]
                                + [f["L1_attn_w_sigma"]])),
        freq=c(np.tile(f["L0_attn_omega"].T, (4, 1))),
        wq0=heads(f["L0_attn_Wq"], (0, 1)), wk0=heads(f["L0_attn_Wk"], (0, 1)),
        wvT0=c(f["L0_attn_Wv"].T.reshape(2, H0, DH0, D).transpose(0, 2, 1, 3).reshape(128, H0, D)),
        wo0=c(f["L0_attn_Wo"].reshape(2, H0, DH0, D).transpose(0, 2, 1, 3).reshape(128, H0, D)),
        gate_w=spread(f["L0_xattn_igate_w"], f["L0_xattn_fgate_w"], (H1, 3, D)).transpose(2, 1, 0).copy(),
        gate_b=spread(f["L0_xattn_igate_b"], f["L0_xattn_fgate_b"], (H1, 1)),
        ln_scale=tile(f["L0_xattn_ln_scale"]),
        sel24=c(np.broadcast_to(-1.0 * (np.arange(72)[:, None] % 32 == e)[:, :, None], (72, 8, 128)).astype(f32)),
        gw0=c(f["L0_ffn_gate_w"]), gate_b0=tile(f["L0_ffn_gate_b"]),
        w_up=c(np.concatenate([f["L0_ffn_sh_w1"][None], f["L0_ffn_ew1"]]).transpose(1, 0, 2)),
        b_up=c(np.concatenate([f["L0_ffn_sh_b1"][None], f["L0_ffn_eb1"]]).reshape(E0S, CH, 128).transpose(2, 0, 1)),
        w_down=c(np.concatenate([f["L0_ffn_sh_w2"][None], f["L0_ffn_ew2"]])
                 .reshape(E0S, CH, 128, D).transpose(2, 0, 1, 3)),
        b_sh=tile(f["L0_ffn_sh_b2"]), b_down=c(f["L0_ffn_eb2"]),
        wq2=c(np.concatenate([f["L1_attn_Wqt"], f["L1_attn_Wqs"]], 1)),
        wk2=c(np.concatenate([f["L1_attn_Wkt"], f["L1_attn_Wks"]], 1)),
        wv2=c(f["L1_attn_Wv"]), wout2=c(f["L1_attn_Wout"]), bout=tile(f["L1_attn_bout"]),
        w1x=c(f["L1_xattn_W"][:, :D].T), w2x=c(f["L1_xattn_W"][:, D:].T), xb=tile(f["L1_xattn_b"]),
        gw1=c(f["L1_ffn_gate_w"].T), lb_bias=tile(f["L1_ffn_lb_bias"]),
        w_g1=c(np.concatenate([f["L1_ffn_expert_gate_w"].reshape(E1 * I1, D), f["L1_ffn_shared_gate_w"]])
               .reshape(BLK, 128, D).transpose(2, 0, 1)),
        w_u1=c(np.concatenate([f["L1_ffn_expert_up_w"].reshape(E1 * I1, D), f["L1_ffn_shared_up_w"]])
               .reshape(BLK, 128, D).transpose(2, 0, 1)),
        w_d1=c(np.concatenate([f["L1_ffn_expert_down_w"].transpose(0, 2, 1).reshape(E1 * I1, D),
                               f["L1_ffn_shared_down_w"].T]).reshape(BLK, 128, D).transpose(1, 0, 2)),
        sel2=c(np.broadcast_to((e[:, None, None] == (2 * np.arange(PAIRS)[:, None] + (i // 64))), (8, PAIRS, 128))
               .astype(f32)),
    )
    return a


def kernel(**inputs):
    import concourse.bacc as bacc
    from concourse.bass_utils import run_bass_kernel_spmd as run

    fp32 = mybir.dt.float32
    arrays = layouts(inputs)
    nc = bacc.Bacc("TRN2", target_bir_lowering=False, num_devices=1)
    aps = {k: nc.dram_tensor("in_" + k, v.shape, fp32, kind="ExternalInput").ap() for k, v in arrays.items()}
    out = nc.dram_tensor("out", (B, N, D), fp32, kind="ExternalOutput").ap()
    x5 = nc.dram_tensor("x5_scratch", (G, 128, W), fp32, kind="Internal").ap()
    x5T = nc.dram_tensor("x5T_scratch", (G, 128, W), fp32, kind="Internal").ap()
    decoder(nc, aps, out.rearrange("(g b) t d -> g b t d", b=GB), x5, x5T)
    r = run(nc, [{"in_" + k: v for k, v in arrays.items()}], core_ids=[0])
    return r.results[0]["out"]
```
